# Optimizing a Trainium2 kernel written in Bass

```python
import numpy as np
import jax
import jax.numpy as jnp

def _softmax(x, axis=-1):
    return jax.nn.softmax(x, axis=axis)

def _gelu(x):
    return jax.nn.gelu(x, approximate=True)

def _silu(x):
    return jax.nn.silu(x)

def _sigmoid(x):
    return jax.nn.sigmoid(x)

def _layernorm(x, axis=-1, eps=1e-05):
    m = jnp.mean(x, axis=axis, keepdims=True)
    v = jnp.var(x, axis=axis, keepdims=True)
    return (x - m) / jnp.sqrt(v + eps)

def _scatter_add(tgt, idx, src, axis=0):
    return tgt.at[idx].add(src)

def _segment_sum(src, seg, n):
    return jax.ops.segment_sum(src, seg, n)
kernel_name = 'mk_adaln_ffn_d2_seqx_r8_783531'

def setup_inputs(seed: int=0):
    np.random.seed(seed)
    _w = jnp.asarray

    def _rec_inputs():
        import jax
        import jax.numpy as jnp
        _rk = jax.random.key(seed)
        x = -0.000125 + 0.9999 * jax.random.normal(jax.random.fold_in(_rk, 1), (4, 256, 256), jnp.float32)
        _lenS = 256 - jax.random.randint(jax.random.fold_in(_rk, 7), (4,), 0, max(1, 256 // 4) + 1, jnp.int32)
        _lenS2 = 256 - jax.random.randint(jax.random.fold_in(_rk, 8), (4,), 0, max(1, 256 // 4) + 1, jnp.int32)
        fside_BxSxS_0 = -1.52775e-05 + 0.999936 * jax.random.normal(jax.random.fold_in(_rk, 11), (4, 256, 256), jnp.float32)
        cond_512 = -5.03954e-05 + 1.00559 * jax.random.normal(jax.random.fold_in(_rk, 12), (4, 64), jnp.float32)
        return (x, fside_BxSxS_0, cond_512)
    x, fside_BxSxS_0, cond_512 = _rec_inputs()

    def _L0_cond_setup():
        import jax, jax.numpy as jnp
        from jax import lax
        import numpy as np
        B, T, C, TD = (8, 256, 256, 64)

        def _bi_wkv(r, k, v, w, u, time_emb):
            tf = jax.nn.sigmoid(jnp.sum(time_emb, axis=-1))[:, None, None]
            decay = jnp.exp(-jnp.exp(w.astype(jnp.float32)))[None, :] * (0.5 + 0.5 * tf[:, :, 0])
            kf = k.astype(jnp.float32)
            vf = v.astype(jnp.float32)
            ek = jnp.exp(jnp.minimum(kf, 30.0))
            ekv = ek * vf

            def step(carry, x):
                a, b = carry
                ekv_t, ek_t = x
                a = a * decay + ekv_t
                b = b * decay + ek_t
                return ((a, b), (a, b))
            ekv_t = jnp.swapaxes(ekv, 0, 1)
            ek_t = jnp.swapaxes(ek, 0, 1)
            init = (jnp.zeros_like(decay), jnp.zeros_like(decay))
            _, (nf, df) = lax.scan(step, init, (ekv_t, ek_t))
            _, (nb, db) = lax.scan(step, init, (ekv_t, ek_t), reverse=True)
            nf = jnp.swapaxes(nf, 0, 1)
            df = jnp.swapaxes(df, 0, 1)
            nb = jnp.swapaxes(nb, 0, 1)
            db = jnp.swapaxes(db, 0, 1)
            euk = jnp.exp(jnp.minimum(u.astype(jnp.float32)[None, None, :] + kf, 30.0))
            num = nf + nb - ekv + euk * vf
            den = df + db - ek + euk
            base = jax.nn.sigmoid(r.astype(jnp.float32)) * (num / jnp.maximum(den, 1e-08))
            out = base * (0.8 + 0.2 * tf)
            return out.astype(r.dtype)
        key = jax.random.key(seed)
        ks = jax.random.split(key, 6)
        return {'r': jax.random.normal(ks[0], (B, T, C), dtype=jnp.float32), 'k': jax.random.normal(ks[1], (B, T, C), dtype=jnp.float32), 'v': jax.random.normal(ks[2], (B, T, C), dtype=jnp.float32), 'w': jax.random.normal(ks[3], (C,), dtype=jnp.float32), 'u': jax.random.normal(ks[4], (C,), dtype=jnp.float32), 'time_emb': jax.random.normal(ks[5], (B, TD), dtype=jnp.float32)}
    _L0_cond_all = _L0_cond_setup()
    _L0_cond_in = {k: v for k, v in _L0_cond_all.items() if k in ('w', 'u')}
    del _L0_cond_all

    def _L0_ffn_setup():
        import jax, jax.numpy as jnp
        import numpy as np
        B, S, D = (4, 512, 256)
        E, K, I, J = (8, 2, 176, 704)
        CAP_FACTOR = 1.25
        STD = 0.02

        def _moe_routed(x_flat, router, w_up_gate, w_down):
            T, d = x_flat.shape
            logits = jnp.einsum('td,de->te', x_flat, router)
            topk_logits, sel = jax.lax.top_k(logits, K)
            cw = jax.nn.softmax(topk_logits, axis=-1).astype(x_flat.dtype)
            C = int(np.ceil(T * K / E * CAP_FACTOR))
            e_flat = sel.reshape(-1)
            oh = jax.nn.one_hot(e_flat, E, dtype=jnp.int32)
            pos_all = jnp.cumsum(oh, axis=0) - oh
            pos = jnp.take_along_axis(pos_all, e_flat[:, None], axis=1)[:, 0]
            valid = pos < C
            safe_pos = jnp.where(valid, pos, C)
            tok = jnp.repeat(jnp.arange(T), K)
            buf = jnp.zeros((E, C, d), x_flat.dtype).at[e_flat, safe_pos].set(x_flat[tok], mode='drop')
            gate_up = jnp.einsum('ecd,edm->ecm', buf, w_up_gate)
            gate, up = jnp.split(gate_up, [I], axis=-1)
            h = jax.nn.silu(gate) * up
            out_buf = jnp.einsum('eci,eid->ecd', h, w_down)
            gathered = out_buf[e_flat, jnp.minimum(safe_pos, C - 1)]
            gathered = gathered * valid[:, None].astype(x_flat.dtype)
            w = cw.reshape(-1)
            y = jnp.zeros((T, d), x_flat.dtype).at[tok].add(w[:, None] * gathered)
            return y

        def _shared_mlp(x_flat, shared_w_up_gate, shared_w_down):
            gu = jnp.einsum('td,dm->tm', x_flat, shared_w_up_gate)
            gate, up = jnp.split(gu, [J], axis=-1)
            return jnp.einsum('tm,md->td', jax.nn.silu(gate) * up, shared_w_down)
        key = jax.random.key(seed)
        kx, kr, ku, kd, ksu, ksd = jax.random.split(key, 6)
        x = jax.random.normal(kx, (B, S, D), dtype=jnp.float32)
        router = STD * jax.random.truncated_normal(kr, -3, 3, (D, E), dtype=jnp.float32)
        w_up_gate = STD * jax.random.truncated_normal(ku, -3, 3, (E, D, 2 * I), dtype=jnp.float32)
        w_down = STD * jax.random.truncated_normal(kd, -3, 3, (E, I, D), dtype=jnp.float32)
        shared_w_up_gate = STD * jax.random.truncated_normal(ksu, -3, 3, (D, 2 * J), dtype=jnp.float32)
        shared_w_down = STD * jax.random.truncated_normal(ksd, -3, 3, (J, D), dtype=jnp.float32)
        return {'x': x, 'router': router, 'w_up_gate': w_up_gate, 'w_down': w_down, 'shared_w_up_gate': shared_w_up_gate, 'shared_w_down': shared_w_down}
    _L0_ffn_all = _L0_ffn_setup()
    _L0_ffn_in = {k: v for k, v in _L0_ffn_all.items() if k in ('router', 'w_up_gate', 'w_down', 'shared_w_up_gate', 'shared_w_down')}
    del _L0_ffn_all

    def _L1_cond_setup():
        import jax, jax.numpy as jnp
        from jax import lax
        import numpy as np
        B, T, C, TD = (8, 256, 256, 64)

        def _bi_wkv(r, k, v, w, u, time_emb):
            tf = jax.nn.sigmoid(jnp.sum(time_emb, axis=-1))[:, None, None]
            decay = jnp.exp(-jnp.exp(w.astype(jnp.float32)))[None, :] * (0.5 + 0.5 * tf[:, :, 0])
            kf = k.astype(jnp.float32)
            vf = v.astype(jnp.float32)
            ek = jnp.exp(jnp.minimum(kf, 30.0))
            ekv = ek * vf

            def step(carry, x):
                a, b = carry
                ekv_t, ek_t = x
                a = a * decay + ekv_t
                b = b * decay + ek_t
                return ((a, b), (a, b))
            ekv_t = jnp.swapaxes(ekv, 0, 1)
            ek_t = jnp.swapaxes(ek, 0, 1)
            init = (jnp.zeros_like(decay), jnp.zeros_like(decay))
            _, (nf, df) = lax.scan(step, init, (ekv_t, ek_t))
            _, (nb, db) = lax.scan(step, init, (ekv_t, ek_t), reverse=True)
            nf = jnp.swapaxes(nf, 0, 1)
            df = jnp.swapaxes(df, 0, 1)
            nb = jnp.swapaxes(nb, 0, 1)
            db = jnp.swapaxes(db, 0, 1)
            euk = jnp.exp(jnp.minimum(u.astype(jnp.float32)[None, None, :] + kf, 30.0))
            num = nf + nb - ekv + euk * vf
            den = df + db - ek + euk
            base = jax.nn.sigmoid(r.astype(jnp.float32)) * (num / jnp.maximum(den, 1e-08))
            out = base * (0.8 + 0.2 * tf)
            return out.astype(r.dtype)
        key = jax.random.key(seed)
        ks = jax.random.split(key, 6)
        return {'r': jax.random.normal(ks[0], (B, T, C), dtype=jnp.float32), 'k': jax.random.normal(ks[1], (B, T, C), dtype=jnp.float32), 'v': jax.random.normal(ks[2], (B, T, C), dtype=jnp.float32), 'w': jax.random.normal(ks[3], (C,), dtype=jnp.float32), 'u': jax.random.normal(ks[4], (C,), dtype=jnp.float32), 'time_emb': jax.random.normal(ks[5], (B, TD), dtype=jnp.float32)}
    _L1_cond_all = _L1_cond_setup()
    _L1_cond_in = {k: v for k, v in _L1_cond_all.items() if k in ('w', 'u')}
    del _L1_cond_all

    def _L1_ffn_setup():
        import jax, jax.numpy as jnp
        import numpy as np
        DIM = 256
        N_EXPERTS = 8
        TOP_K = 2
        key = jax.random.key(seed)
        ks = jax.random.split(key, 5)
        x = jax.random.normal(ks[0], (4, 512, DIM), dtype=jnp.float32)
        W_up = jax.random.normal(ks[1], (DIM, DIM), dtype=jnp.float32) * (1.0 / np.sqrt(DIM))
        W_down = jax.random.normal(ks[2], (DIM, DIM), dtype=jnp.float32) * (1.0 / np.sqrt(DIM))
        W_gate = jax.random.normal(ks[3], (N_EXPERTS, DIM), dtype=jnp.float32) * (1.0 / np.sqrt(DIM))
        W_expert = jax.random.normal(ks[4], (DIM, DIM), dtype=jnp.float32) * (1.0 / np.sqrt(DIM))
        return {'x': x, 'W_up': W_up, 'W_down': W_down, 'W_gate': W_gate, 'W_expert': W_expert}
    _L1_ffn_all = _L1_ffn_setup()
    _L1_ffn_in = {k: v for k, v in _L1_ffn_all.items() if k in ('W_up', 'W_down', 'W_gate', 'W_expert')}
    del _L1_ffn_all
    return {'x': x, 'fside_BxSxS_0': fside_BxSxS_0, 'cond_512': cond_512, 'L0_cond_w': _L0_cond_in['w'], 'L0_cond_u': _L0_cond_in['u'], 'L0_ffn_router': _L0_ffn_in['router'], 'L0_ffn_w_up_gate': _L0_ffn_in['w_up_gate'], 'L0_ffn_w_down': _L0_ffn_in['w_down'], 'L0_ffn_shared_w_up_gate': _L0_ffn_in['shared_w_up_gate'], 'L0_ffn_shared_w_down': _L0_ffn_in['shared_w_down'], 'L1_cond_w': _L1_cond_in['w'], 'L1_cond_u': _L1_cond_in['u'], 'L1_ffn_W_up': _L1_ffn_in['W_up'], 'L1_ffn_W_down': _L1_ffn_in['W_down'], 'L1_ffn_W_gate': _L1_ffn_in['W_gate'], 'L1_ffn_W_expert': _L1_ffn_in['W_expert']}

def reference(x, fside_BxSxS_0, cond_512, L0_cond_w, L0_cond_u, L0_ffn_router, L0_ffn_w_up_gate, L0_ffn_w_down, L0_ffn_shared_w_up_gate, L0_ffn_shared_w_down, L1_cond_w, L1_cond_u, L1_ffn_W_up, L1_ffn_W_down, L1_ffn_W_gate, L1_ffn_W_expert):
    import jax
    import jax.numpy as jnp

    def _L0_cond_ref(r, k, v, w, u, time_emb):
        import jax, jax.numpy as jnp
        from jax import lax
        import numpy as np
        B, T, C, TD = (8, 256, 256, 64)

        def _bi_wkv(r, k, v, w, u, time_emb):
            tf = jax.nn.sigmoid(jnp.sum(time_emb, axis=-1))[:, None, None]
            decay = jnp.exp(-jnp.exp(w.astype(jnp.float32)))[None, :] * (0.5 + 0.5 * tf[:, :, 0])
            kf = k.astype(jnp.float32)
            vf = v.astype(jnp.float32)
            ek = jnp.exp(jnp.minimum(kf, 30.0))
            ekv = ek * vf

            def step(carry, x):
                a, b = carry
                ekv_t, ek_t = x
                a = a * decay + ekv_t
                b = b * decay + ek_t
                return ((a, b), (a, b))
            ekv_t = jnp.swapaxes(ekv, 0, 1)
            ek_t = jnp.swapaxes(ek, 0, 1)
            init = (jnp.zeros_like(decay), jnp.zeros_like(decay))
            _, (nf, df) = lax.scan(step, init, (ekv_t, ek_t))
            _, (nb, db) = lax.scan(step, init, (ekv_t, ek_t), reverse=True)
            nf = jnp.swapaxes(nf, 0, 1)
            df = jnp.swapaxes(df, 0, 1)
            nb = jnp.swapaxes(nb, 0, 1)
            db = jnp.swapaxes(db, 0, 1)
            euk = jnp.exp(jnp.minimum(u.astype(jnp.float32)[None, None, :] + kf, 30.0))
            num = nf + nb - ekv + euk * vf
            den = df + db - ek + euk
            base = jax.nn.sigmoid(r.astype(jnp.float32)) * (num / jnp.maximum(den, 1e-08))
            out = base * (0.8 + 0.2 * tf)
            return out.astype(r.dtype)
        return _bi_wkv(r, k, v, w, u, time_emb)

    def _L0_ffn_ref(x, router, w_up_gate, w_down, shared_w_up_gate, shared_w_down):
        import jax, jax.numpy as jnp
        import numpy as np
        B, S, D = (4, 512, 256)
        E, K, I, J = (8, 2, 176, 704)
        CAP_FACTOR = 1.25
        STD = 0.02

        def _moe_routed(x_flat, router, w_up_gate, w_down):
            T, d = x_flat.shape
            logits = jnp.einsum('td,de->te', x_flat, router)
            topk_logits, sel = jax.lax.top_k(logits, K)
            cw = jax.nn.softmax(topk_logits, axis=-1).astype(x_flat.dtype)
            C = int(np.ceil(T * K / E * CAP_FACTOR))
            e_flat = sel.reshape(-1)
            oh = jax.nn.one_hot(e_flat, E, dtype=jnp.int32)
            pos_all = jnp.cumsum(oh, axis=0) - oh
            pos = jnp.take_along_axis(pos_all, e_flat[:, None], axis=1)[:, 0]
            valid = pos < C
            safe_pos = jnp.where(valid, pos, C)
            tok = jnp.repeat(jnp.arange(T), K)
            buf = jnp.zeros((E, C, d), x_flat.dtype).at[e_flat, safe_pos].set(x_flat[tok], mode='drop')
            gate_up = jnp.einsum('ecd,edm->ecm', buf, w_up_gate)
            gate, up = jnp.split(gate_up, [I], axis=-1)
            h = jax.nn.silu(gate) * up
            out_buf = jnp.einsum('eci,eid->ecd', h, w_down)
            gathered = out_buf[e_flat, jnp.minimum(safe_pos, C - 1)]
            gathered = gathered * valid[:, None].astype(x_flat.dtype)
            w = cw.reshape(-1)
            y = jnp.zeros((T, d), x_flat.dtype).at[tok].add(w[:, None] * gathered)
            return y

        def _shared_mlp(x_flat, shared_w_up_gate, shared_w_down):
            gu = jnp.einsum('td,dm->tm', x_flat, shared_w_up_gate)
            gate, up = jnp.split(gu, [J], axis=-1)
            return jnp.einsum('tm,md->td', jax.nn.silu(gate) * up, shared_w_down)
        b, s, d = x.shape
        x_flat = x.reshape(b * s, d)
        routed = _moe_routed(x_flat, router, w_up_gate, w_down)
        shared = _shared_mlp(x_flat, shared_w_up_gate, shared_w_down)
        return (routed + shared).reshape(b, s, d)

    def _L1_cond_ref(r, k, v, w, u, time_emb):
        import jax, jax.numpy as jnp
        from jax import lax
        import numpy as np
        B, T, C, TD = (8, 256, 256, 64)

        def _bi_wkv(r, k, v, w, u, time_emb):
            tf = jax.nn.sigmoid(jnp.sum(time_emb, axis=-1))[:, None, None]
            decay = jnp.exp(-jnp.exp(w.astype(jnp.float32)))[None, :] * (0.5 + 0.5 * tf[:, :, 0])
            kf = k.astype(jnp.float32)
            vf = v.astype(jnp.float32)
            ek = jnp.exp(jnp.minimum(kf, 30.0))
            ekv = ek * vf

            def step(carry, x):
                a, b = carry
                ekv_t, ek_t = x
                a = a * decay + ekv_t
                b = b * decay + ek_t
                return ((a, b), (a, b))
            ekv_t = jnp.swapaxes(ekv, 0, 1)
            ek_t = jnp.swapaxes(ek, 0, 1)
            init = (jnp.zeros_like(decay), jnp.zeros_like(decay))
            _, (nf, df) = lax.scan(step, init, (ekv_t, ek_t))
            _, (nb, db) = lax.scan(step, init, (ekv_t, ek_t), reverse=True)
            nf = jnp.swapaxes(nf, 0, 1)
            df = jnp.swapaxes(df, 0, 1)
            nb = jnp.swapaxes(nb, 0, 1)
            db = jnp.swapaxes(db, 0, 1)
            euk = jnp.exp(jnp.minimum(u.astype(jnp.float32)[None, None, :] + kf, 30.0))
            num = nf + nb - ekv + euk * vf
            den = df + db - ek + euk
            base = jax.nn.sigmoid(r.astype(jnp.float32)) * (num / jnp.maximum(den, 1e-08))
            out = base * (0.8 + 0.2 * tf)
            return out.astype(r.dtype)
        return _bi_wkv(r, k, v, w, u, time_emb)

    def _L1_ffn_ref(x, W_up, W_down, W_gate, W_expert):
        import jax, jax.numpy as jnp
        import numpy as np
        DIM = 256
        N_EXPERTS = 8
        TOP_K = 2
        logits = jnp.einsum('bsd,ed->bse', x, W_gate)
        routing_weights, selected_experts = jax.lax.top_k(logits, TOP_K)
        shared_out = jnp.einsum('bsd,od->bso', jax.nn.relu(jnp.einsum('bsd,od->bso', x, W_up)), W_down)
        rw = jax.nn.softmax(routing_weights, axis=-1)
        expert_out = jnp.einsum('bsd,do->bso', x, W_expert)
        moe_out = jnp.sum(rw, axis=-1, keepdims=True) * expert_out
        return shared_out + moe_out
    x = x + _L0_ffn_ref(_L0_cond_ref(x, fside_BxSxS_0, fside_BxSxS_0, L0_cond_w, L0_cond_u, cond_512), L0_ffn_router, L0_ffn_w_up_gate, L0_ffn_w_down, L0_ffn_shared_w_up_gate, L0_ffn_shared_w_down)
    x = x + _L1_ffn_ref(_L1_cond_ref(x, fside_BxSxS_0, fside_BxSxS_0, L1_cond_w, L1_cond_u, cond_512), L1_ffn_W_up, L1_ffn_W_down, L1_ffn_W_gate, L1_ffn_W_expert)
    return x

_drawn_inputs = setup_inputs


def setup_inputs(seed=0):
    import zlib

    import numpy as np

    out = dict(_drawn_inputs(seed))
    spreads = {}
    factors = {'L0_cond_w': 8.0,
     'L0_cond_u': 8.0,
     'L0_ffn_router': 8.0,
     'L0_ffn_w_up_gate': 8.0,
     'L0_ffn_w_down': 8.0,
     'L0_ffn_shared_w_up_gate': 8.0,
     'L0_ffn_shared_w_down': 8.0,
     'L1_ffn_W_gate': 64.0,
     'L1_cond_u': 3.453}
    for name, (base, spread) in spreads.items():
        noise = np.random.default_rng([zlib.crc32(name.encode()), seed]).standard_normal(out[name].shape)
        drawn = base * np.exp(spread * noise) if base else spread * noise
        out[name] = jnp.asarray(drawn.astype(out[name].dtype))
    for name, factor in factors.items():
        out[name] = (out[name] * factor).astype(out[name].dtype)
    return out
```

```python
from contextlib import ExitStack

import concourse.bass as bass
from concourse import mybir

F32 = mybir.dt.float32
BF16 = mybir.dt.bfloat16
U32 = mybir.dt.uint32
ALU = mybir.AluOpType
ACT = mybir.ActivationFunctionType
AX = mybir.AxisListType

P = 128
B, T, C = 4, 256, 256
CH = C // P
NT = B * T // P
TB = T // P
E, CAP = 8, 320
I, J = 176, 704
IA = 112
IB = I - IA
JC = J // P
JR = J - JC * P
SLOTS = E * CAP
EXP30 = 10686474581524.463
ROUNDS = ((0, 3), (3, 4))
NCHUNK = JC + 1
RANK_AT = 3


def adaln_ffn(nc, x_cm, x_tm, k_cm, cond, wu, router, sup, sdn, mup, mdn, l1w, l1g, out):
    slots_in = nc.dram_tensor("slots_in", (SLOTS, C), F32).ap()
    slots_out = nc.dram_tensor("slots_out", (SLOTS, C), F32).ap()

    with ExitStack() as ctx:
        def sb(name, shape, dt=F32):
            return ctx.enter_context(nc.sbuf_tensor(name, shape, dt))

        def sem(name):
            return ctx.enter_context(nc.semaphore(name))

        def sems(name, n):
            return [sem(f"{name}{i}") for i in range(n)]

        k = sb("k", [P, B, CH, T])
        xc = sb("xc", [P, B, CH, T])
        xt = sb("xt", [P, NT, C])
        ek = sb("ek", [P, B, CH, T])
        ekv = sb("ekv", [P, B, CH, T])
        euk = sb("euk", [P, 2, B, CH, T])
        nf = sb("nf", [P, CH, T])
        nb = sb("nb", [P, CH, T + 1])
        df = sb("df", [P, CH, T])
        db = sb("db", [P, CH, T + 1])
        euv = sb("euv", [P, CH, T])
        htok = sb("htok", [P, NT, C])
        wu_s = sb("wu_s", [P, 4, CH])
        cond_s = sb("cond_s", [P, B, 64])
        zsum = sb("zsum", [P, B])
        gate_t = sb("gate_t", [P, 3, B])
        halfp = sb("halfp", [P, B])
        oscale = sb("oscale", [P, B])
        ew = sb("ew", [P, 2, 2, CH])
        decay = sb("decay", [P, 2, B, CH])
        router_s = sb("router_s", [P, CH, E])
        sup_s = sb("sup_s", [P, CH * 2 * J])
        sdn_s = sb("sdn_s", [P, NCHUNK, C])
        mup_s = sb("mup_s", [P, E, CH, 2 * I])
        mdn_s = sb("mdn_s", [IA, E, 2, C])
        l1_s = sb("l1_s", [P, 3, CH, C])
        l1g_s = sb("l1g_s", [P, CH, E])
        ident = sb("ident", [P, P])
        before = sb("before", [P, P], BF16)
        ones = sb("ones", [P, P], BF16)
        iota_e = sb("iota_e", [P, E])
        zero = sb("zero", [P, 512])
        gate_a = sb("gate_a", [P, 2, CAP])
        hid = sb("hid", [P, 2, NCHUNK, T])
        buf = sb("buf", [P, 2, 5, C])
        bufT = sb("bufT", [P, 2, CH, 2 * CAP])
        hidm = sb("hidm", [IA, 2, 2, CAP])
        outb = sb("outb", [P, 2, 3, C])
        got = ek[:].rearrange("p b c t -> p (b c t)").rearrange("p (k n d) -> p k n d", k=2, n=TB * 2)
        got2 = ekv[:].rearrange("p b c t -> p (b c t)").rearrange("p (k n d) -> p k n d", k=2, n=TB * 2)
        lg = sb("lg", [P, NT, E])
        lgm = sb("lgm", [P, NT, E])
        eq = sb("eq", [P, NT, E])
        cand = sb("cand", [P, 2, NT, E])
        oh = sb("oh", [P, 2, NT, E])
        hot = sb("hot", [P, NT, E], BF16)
        ohp = sb("ohp", [P, 2, NT, E])
        top = sb("top", [P, 2, NT])
        first = sb("first", [P, 2, NT])
        eidx = sb("eidx", [P, 2, NT])
        pos = sb("pos", [P, 2, NT])
        posc = sb("posc", [P, 2, NT])
        over = sb("over", [P, 2, NT])
        slot = sb("slot", [P, 2, NT])
        valid = sb("valid", [P, 2, NT])
        put_at = sb("put_at", [P, 2, NT], U32)
        get_at = sb("get_at", [P, 2, NT], U32)
        dtop = sb("dtop", [P, NT])
        dth = sb("dth", [P, NT])
        cw = sb("cw", [P, 2, NT])
        h1 = sb("h1", [P, 2, CH, T])
        hid1 = sb("hid1", [P, 2, CH, T])
        top1 = sb("top1", [P, B, TB, 8])
        dtop1 = sb("dtop1", [P, B, TB])
        dth1 = sb("dth1", [P, B, TB])
        rw = sb("rw", [P, B, 3, TB])

        def bank(name):
            return ctx.enter_context(nc.psum_tensor(name, [P, 512], F32))

        hb = [bank(f"hb{i}") for i in range(4)]
        dn = [bank(f"dn{i}") for i in range(2)]
        tp = [bank(f"tp{i}") for i in range(2)]

        chunk_banks, unit = [], 0
        for n in [1] * (B * NCHUNK) + [2, 1] * E:
            chunk_banks.append([(unit + i) % 4 for i in range(n)])
            unit += n
        nshared = B * NCHUNK
        nchunks = len(chunk_banks)

        def chunk_before(c):
            need = 0
            for b_ in chunk_banks[c]:
                last = max((i for i in range(c) if b_ in chunk_banks[i]), default=-1)
                need = max(need, last + 1)
            return need

        ld_k, ld_x = sems("ld_k", B), sems("ld_x", B)
        ld_small, ld_cond, ld_router = sem("ld_small"), sem("ld_cond"), sem("ld_router")
        ld_sup, ld_sdn, ld_xt = sems("ld_sup", 3), sem("ld_sdn"), sem("ld_xt")
        ld_mup, ld_mdn = sems("ld_mup", 4), sem("ld_mdn")
        ld_l1 = sem("ld_l1")
        consts = sem("consts")
        zeroed = sem("zeroed")
        exp_done = sem("exp_done")
        tanh_done = sem("tanh_done")
        vec = sem("vec")
        h0_ready = sem("h0_ready")
        htp_ready = sem("htp_ready")
        htok_ready = sem("htok_ready")
        lg_ready = sem("lg_ready")
        hot_ready = sem("hot_ready")
        pos_ready = sem("pos_ready")
        dtop_ready = sem("dtop_ready")
        dth_ready = sem("dth_ready")
        put_ready = sem("put_ready")
        routed = sem("routed")
        up_ready = sem("up_ready")
        silu_ready = sem("silu_ready")
        hid_ready = sem("hid_ready")
        sh_ready = sem("sh_ready")
        sh_taken = sem("sh_taken")
        scattered = sem("scattered")
        ld_buf = sems("ld_buf", E // 2)
        btp_ready = sem("btp_ready")
        bufT_ready = sem("bufT_ready")
        mo_ready = sem("mo_ready")
        mo_taken = sem("mo_taken")
        written = sems("written", 2)
        q1_ready = sem("q1_ready")
        gathered = sems("gathered", B)
        x1_ready = sem("x1_ready")
        x1T_ready = sem("x1T_ready")
        tanh1_done = sem("tanh1_done")
        h1_ready = sem("h1_ready")
        up1_ready = sem("up1_ready")
        relu_done = sem("relu_done")
        gate1_ready = sem("gate1_ready")
        dtop1_ready = sem("dtop1_ready")
        dth1_ready = sem("dth1_ready")
        y_ready = sem("y_ready")
        y_done = sem("y_done")
        stored = sem("stored")

        block = ctx.enter_context(nc.Block())

        def got_of(b, j, i):
            g = got if b < 2 else got2
            return g[:, j, (b % 2) * TB + i]

        def store_expert(sp, e):
            sp.wait_ge(mo_taken, 2 * (e + 1))
            rows = slots_out[e * CAP:(e + 1) * CAP]
            sp.dma_start(rows[0:2 * P].rearrange("(r p) d -> p r d", p=P), outb[:, e % 2, 0:2]).then_inc(written[e % 2], 16)
            sp.dma_start(rows[2 * P:CAP], outb[0:CAP - 2 * P, e % 2, 2]).then_inc(written[e % 2], 16)

        def ranks(pe, mm, r):
            b0, b1 = ROUNDS[r]
            n0, n1 = b0 * TB, b1 * TB
            pe.wait_ge(hot_ready, r + 1)
            dst = tp[1][:, 64 + n0 * E:64 + n1 * E]
            last = mm(dst, before[:], hot[:, n0:n1], True, n1 == 1)
            for n in range(n1 - 1):
                lo = max(n + 1, n0)
                last = mm(tp[1][:, 64 + lo * E:64 + n1 * E], ones[:], hot[:, n:n + 1].to_broadcast([P, n1 - lo, E]), False, n == n1 - 2)
            last.then_inc(pos_ready, 1)

        @block.sync
        def _(sp):
            sp.dma_start(wu_s[:], wu).then_inc(ld_small, 16)
            sp.dma_start(k[:, 0], k_cm[:, 0]).then_inc(ld_k[0], 16)
            sp.dma_start(cond_s[:], cond.unsqueeze(0).to_broadcast([P, B, 64])).then_inc(ld_cond, 16)
            sp.dma_start(xc[:, 0], x_cm[:, 0]).then_inc(ld_x[0], 16)
            sp.dma_start(router_s[:], router).then_inc(ld_router, 16)
            for b in range(1, B):
                sp.dma_start(k[:, b], k_cm[:, b]).then_inc(ld_k[b], 16)
            sp.dma_start(xc[:, 1], x_cm[:, 1]).then_inc(ld_x[1], 16)
            for i, (a, z) in enumerate(((0, 1024), (1024, 2048), (2048, 2 * CH * J))):
                sp.dma_start(sup_s[:, a:z], sup[:, a:z]).then_inc(ld_sup[i], 16)
            sp.dma_start(xc[:, 2], x_cm[:, 2]).then_inc(ld_x[2], 16)
            sp.dma_start(sdn_s[:, 0:JC], sdn[0:JC * P].rearrange("(j p) d -> p j d", p=P)).then_inc(ld_sdn, 16)
            sp.dma_start(sdn_s[0:JR, JC], sdn[JC * P:J]).then_inc(ld_sdn, 16)
            sp.dma_start(xc[:, 3], x_cm[:, 3]).then_inc(ld_x[3], 16)
            sp.dma_start(xt[:], x_tm).then_inc(ld_xt, 16)
            sp.wait_ge(consts, 1)
            for i in range(10):
                sp.dma_start(slots_in[i * 256:(i + 1) * 256].rearrange("(p r) d -> p (r d)", r=2),
                             zero[:]).then_inc(zeroed, 16)
            for i in range(4):
                sp.dma_start(mup_s[:, 2 * i:2 * i + 2], mup[:, 2 * i:2 * i + 2]).then_inc(ld_mup[i], 16)
                if i == 0:
                    sp.dma_start(mdn_s[:, :, 0], mdn[:, 0:IA].rearrange("e i d -> i e d")).then_inc(ld_mdn, 16)
                    sp.dma_start(mdn_s[0:IB, :, 1], mdn[:, IA:I].rearrange("e i d -> i e d")).then_inc(ld_mdn, 16)
            sp.dma_start(l1_s[:], l1w).then_inc(ld_l1, 16)
            sp.dma_start(l1g_s[:], l1g).then_inc(ld_l1, 16)
            sp.wait_ge(scattered, 16 * 2 * NT)
            for q in range(E // 2):
                if q >= 2:
                    sp.wait_ge(btp_ready, 3 * (q - 1))
                sp.dma_start(buf[:, q % 2], slots_in[q * 640:(q + 1) * 640].rearrange("(r p) d -> p r d", p=P)).then_inc(ld_buf[q], 16)
                if q >= 1:
                    store_expert(sp, 2 * q - 2)
                    store_expert(sp, 2 * q - 1)
            store_expert(sp, E - 2)
            store_expert(sp, E - 1)
            for n in range(NT):
                sp.wait_ge(y_done, n + 1)
                sp.dma_start(out[n * P:(n + 1) * P], xt[:, n]).then_inc(stored, 16)
            sp.wait_ge(stored, 16 * NT)

        @block.gpsimd
        def _(pool):
            nc.gpsimd.memset(zero[:], 0.0).then_inc(consts, 1)
            nc.gpsimd.memset(ident[:], 0.0).then_inc(consts, 1)
            nc.gpsimd.memset(ones[:], 1.0).then_inc(consts, 1)
            for e in range(E):
                nc.gpsimd.memset(iota_e[:, e:e + 1], float(e)).then_inc(consts, 1)
            pool.wait_ge(consts, 3 + E)
            nc.gpsimd.affine_select(out=ident[:], in_=ident[:], compare_op=ALU.not_equal, fill=1.0, base=0,
                                    pattern=[[-1, P]], channel_multiplier=1).then_inc(consts, 1)
            nc.gpsimd.affine_select(out=before[:], in_=ones[:], compare_op=ALU.is_ge, fill=0.0, base=-1,
                                    pattern=[[1, P]], channel_multiplier=-1).then_inc(consts, 1)
            pool.wait_ge(zeroed, 160)
            for r, (b0, b1) in enumerate(ROUNDS):
                pool.wait_ge(put_ready, r + 1)
                pool.wait_ge(htok_ready, b1)
                for n in range(b0 * TB, b1 * TB):
                    for j in range(2):
                        nc.gpsimd.indirect_dma_start(
                            out=slots_in, out_offset=bass.IndirectOffsetOnAxis(ap=put_at[:, j, n:n + 1], axis=0),
                            in_=htok[:, n], in_offset=None, bounds_check=SLOTS - 1, oob_is_err=False).then_inc(scattered, 16)
            pool.wait_ge(written[0], 32 * (E // 2))
            pool.wait_ge(written[1], 32 * (E // 2))
            pool.wait_ge(q1_ready, B)
            pool.wait_ge(routed, len(ROUNDS))
            for b in range(B):
                for i in range(TB):
                    for j in range(2):
                        nc.gpsimd.indirect_dma_start(
                            out=got_of(b, j, i), out_offset=None, in_=slots_out,
                            in_offset=bass.IndirectOffsetOnAxis(ap=get_at[:, j, b * TB + i:b * TB + i + 1], axis=0)).then_inc(gathered[b], 16)

        @block.scalar
        def _(act):
            act.wait_ge(ld_small, 16)
            nc.scalar.activation(ew[:, 0], wu_s[:, 0:2], ACT.Exp).then_inc(exp_done, 1)
            act.wait_ge(exp_done, 1)
            nc.scalar.activation(ew[:, 1], ew[:, 0], ACT.Exp, scale=-1.0).then_inc(exp_done, 1)
            for b in range(B):
                act.wait_ge(ld_k[b], 16)
                nc.scalar.activation(ek[:, b], k[:, b], ACT.Exp).then_inc(exp_done, 1)
                for c in range(CH):
                    nc.scalar.activation(euk[:, 0, b, c], k[:, b, c], ACT.Exp, bias=wu_s[:, 2, c:c + 1]).then_inc(exp_done, 1)
                if b == 0:
                    act.wait_ge(vec, 1)
                    nc.scalar.activation(gate_t[:, 0], zsum[:], ACT.Exp, scale=-1.0).then_inc(exp_done, 1)
            for b in range(B):
                for c in range(CH):
                    nc.scalar.activation(euk[:, 1, b, c], k[:, b, c], ACT.Exp, bias=wu_s[:, 3, c:c + 1]).then_inc(exp_done, 1)
            for b in range(B):
                act.wait_ge(ld_x[b], 16)
                nc.scalar.activation(xc[:, b], xc[:, b], ACT.Tanh, scale=0.5).then_inc(tanh_done, 1)

            def silu(c):
                act.wait_ge(up_ready, c + 1)
                if c >= 2:
                    act.wait_ge(hid_ready, c - 1)
                bank0 = hb[chunk_banks[c][0]]
                if c < nshared:
                    if c % NCHUNK < JC:
                        src, dst = bank0[:, 0:T], gate_a[:, c % 2, 0:T]
                    else:
                        src, dst = bank0[P - JR:P, 0:T], gate_a[0:JR, c % 2, 0:T]
                elif (c - nshared) % 2 == 0:
                    src, dst = bank0[0:IA, 0:CAP], gate_a[0:IA, c % 2]
                else:
                    src, dst = bank0[P - IB:P, 0:CAP], gate_a[0:IB, c % 2]
                nc.scalar.activation(dst, src, ACT.Silu).then_inc(silu_ready, 1)

            def take_bufT(q):
                for i in range(3):
                    act.wait_ge(btp_ready, 3 * q + i + 1)
                    n = min(2, 5 - 2 * i)
                    dst = bufT[:, q % 2, :, 2 * i * P:(2 * i + n) * P]
                    src = tp[(3 * q + i) % 2][:, 0:n * CH * P].rearrange("p (c s) -> p c s", c=CH)
                    nc.scalar.copy(dst, src).then_inc(bufT_ready, 1)

            def take_out(e):
                if e >= 2:
                    act.wait_ge(written[e % 2], 32 * (e // 2))
                act.wait_ge(mo_ready, 2 * e + 1)
                nc.scalar.copy(outb[:, e % 2, 0:2], dn[0][:].rearrange("p (r d) -> p r d", r=2)).then_inc(mo_taken, 1)
                act.wait_ge(mo_ready, 2 * e + 2)
                nc.scalar.copy(outb[0:CAP - 2 * P, e % 2, 2], dn[1][0:CAP - 2 * P, 0:C]).then_inc(mo_taken, 1)

            for b in range(B):
                act.wait_ge(htp_ready, b + 1)
                nc.scalar.copy(htok[:, b * TB:(b + 1) * TB], tp[0][:].rearrange("p (n d) -> p n d", n=TB)).then_inc(htok_ready, 1)
                for j in range(NCHUNK):
                    silu(b * NCHUNK + j)
                    for r, (b0, b1) in enumerate(ROUNDS):
                        if b == b1 - 1 and j == 1:
                            act.wait_ge(dtop_ready, r + 1)
                            nc.scalar.activation(dth[:, b0 * TB:b1 * TB], dtop[:, b0 * TB:b1 * TB], ACT.Tanh, scale=0.5).then_inc(dth_ready, 1)
            take_bufT(0)
            for e in range(E):
                silu(nshared + 2 * e)
                silu(nshared + 2 * e + 1)
                if e % 2 == 1 and e < E - 1:
                    take_bufT((e + 1) // 2)
                if e >= 1:
                    take_out(e - 1)
            take_out(E - 1)
            for b in range(B):
                act.wait_ge(x1T_ready, b + 1)
                if b >= 2:
                    act.wait_ge(up1_ready, b - 1)
                nc.scalar.activation(h1[:, b % 2], tp[0][:].rearrange("p (c t) -> p c t", c=CH), ACT.Tanh, scale=0.5).then_inc(tanh1_done, 1)
                act.wait_ge(up1_ready, b + 1)
                if b >= 2:
                    act.wait_ge(y_ready, TB * (b - 1))
                nc.scalar.activation(hid1[:, b % 2], hb[b % 2][:].rearrange("p (c t) -> p c t", c=CH), ACT.Relu).then_inc(relu_done, 1)
                act.wait_ge(dtop1_ready, b + 1)
                nc.scalar.activation(dth1[:, b], dtop1[:, b], ACT.Tanh, scale=0.5).then_inc(dth1_ready, 1)

        @block.vector
        def _(v):
            ticks = [0]

            def tick(ins):
                ticks[0] += 1
                ins.then_inc(vec, 1)
                return ticks[0]

            def after(n):
                v.wait_ge(vec, n)

            v.wait_ge(ld_cond, 16)
            tick(nc.vector.reduce_sum(zsum[:], cond_s[:], AX.X))
            tick(nc.vector.memset(nb[:, :, T:T + 1], 0.0))
            tick(nc.vector.memset(db[:, :, T:T + 1], 0.0))
            v.wait_ge(exp_done, 2 + 4)
            after(tick(nc.vector.tensor_scalar(gate_t[:, 1], gate_t[:, 0], 1.0, None, ALU.add)))
            after(tick(nc.vector.reciprocal(gate_t[:, 2], gate_t[:, 1])))
            tick(nc.vector.tensor_scalar(halfp[:], gate_t[:, 2], 0.5, 0.5, ALU.mult, ALU.add))
            after(tick(nc.vector.tensor_scalar(oscale[:], gate_t[:, 2], 0.1, 0.4, ALU.mult, ALU.add)))
            for l in range(2):
                for b in range(B):
                    n = tick(nc.vector.tensor_scalar(decay[:, l, b], ew[:, 1, l], halfp[:, b:b + 1], None, ALU.mult))
            after(n)
            h0_taken = [0]

            def wkv(l, b, step):
                eu = euk[:, l, b]
                dec = [decay[:, l, b, c:c + 1] for c in range(CH)]
                if step == 0:
                    if l == 0:
                        v.wait_ge(exp_done, 2 + 3 * (b + 1) + 1)
                        after(tick(nc.vector.tensor_scalar(ek[:, b], ek[:, b], EXP30, None, ALU.min)))
                        tick(nc.vector.tensor_tensor(ekv[:, b], ek[:, b], k[:, b], ALU.mult))
                    else:
                        v.wait_ge(exp_done, 2 + 3 * B + 1 + 2 * (b + 1))
                    after(tick(nc.vector.scalar_tensor_tensor(out=euv[:], in0=eu, scalar=EXP30, in1=k[:, b],
                                                              op0=ALU.min, op1=ALU.mult)))
                elif step in (1, 2):
                    src, fwd, bwd = ((ekv, nf, nb), (ek, df, db))[step - 1]
                    for c in range(CH):
                        d = dec[c].to_broadcast([P, T])
                        tick(nc.vector.tensor_tensor_scan(fwd[:, c], d, src[:, b, c], 0.0, ALU.mult, ALU.add))
                        n = tick(nc.vector.tensor_tensor_scan(rev(bwd[:, c, 0:T]), d,
                                                              rev(src[:, b, c]), 0.0, ALU.mult, ALU.add))
                    after(n)
                elif step == 3:
                    for c in range(CH):
                        n = tick(nc.vector.scalar_tensor_tensor(out=nf[:, c], in0=nb[:, c, 1:T + 1], scalar=dec[c],
                                                                in1=nf[:, c], op0=ALU.mult, op1=ALU.add))
                    after(n)
                    after(tick(nc.vector.tensor_tensor(nf[:], nf[:], euv[:], ALU.add)))
                elif step == 4:
                    for c in range(CH):
                        n = tick(nc.vector.scalar_tensor_tensor(out=df[:, c], in0=db[:, c, 1:T + 1], scalar=dec[c],
                                                                in1=df[:, c], op0=ALU.mult, op1=ALU.add))
                    after(n)
                    after(tick(nc.vector.scalar_tensor_tensor(out=df[:], in0=eu, scalar=EXP30, in1=df[:],
                                                              op0=ALU.min, op1=ALU.add)))
                    after(tick(nc.vector.tensor_scalar(df[:], df[:], 1e-8, None, ALU.max)))
                else:
                    after(tick(nc.vector.reciprocal(df[:], df[:])))
                    if l == 0:
                        after(tick(nc.vector.scalar_tensor_tensor(out=nf[:], in0=nf[:], scalar=oscale[:, b:b + 1],
                                                                  in1=df[:], op0=ALU.mult, op1=ALU.mult)))
                        v.wait_ge(tanh_done, b + 1)
                        nc.vector.scalar_tensor_tensor(out=xc[:, b], in0=xc[:, b], scalar=1.0, in1=nf[:],
                                                       op0=ALU.add, op1=ALU.mult).then_inc(h0_ready, 1)
                        v.wait_ge(h0_ready, b + 1)
                    else:
                        nc.vector.scalar_tensor_tensor(out=eu, in0=nf[:], scalar=oscale[:, b:b + 1],
                                                       in1=df[:], op0=ALU.mult, op1=ALU.mult).then_inc(q1_ready, 1)
                        v.wait_ge(q1_ready, b + 1)

            def hidden(c):
                v.wait_ge(silu_ready, c + 1)
                banks = [hb[i] for i in chunk_banks[c]]
                if c < nshared:
                    b, j = divmod(c, NCHUNK)
                    if b >= 2:
                        v.wait_ge(sh_ready, b - 1)
                    if j < JC:
                        up, g, dst = banks[0][:, T:2 * T], gate_a[:, c % 2, 0:T], hid[:, b % 2, j]
                    else:
                        up, g, dst = banks[0][0:JR, 0:T], gate_a[0:JR, c % 2, 0:T], hid[0:JR, b % 2, j]
                else:
                    e, j = divmod(c - nshared, 2)
                    if e >= 2:
                        v.wait_ge(mo_ready, 2 * (e - 1))
                    if j == 0:
                        up, g, dst = banks[1][0:IA, 0:CAP], gate_a[0:IA, c % 2], hidm[:, e % 2, 0]
                    else:
                        up, g, dst = banks[0][0:IB, 0:CAP], gate_a[0:IB, c % 2], hidm[0:IB, e % 2, 1]
                nc.vector.tensor_tensor(dst, up, g, ALU.mult).then_inc(hid_ready, 1)

            def take_shared(b):
                v.wait_ge(sh_ready, b + 1)
                if b == 0:
                    v.wait_ge(ld_xt, 16)
                t = xt[:, b * TB:(b + 1) * TB]
                nc.vector.tensor_tensor(t, dn[b % 2][:].rearrange("p (n d) -> p n d", n=TB), t, ALU.add).then_inc(sh_taken, 1)

            def route(r):
                b0, b1 = ROUNDS[r]
                s = slice(b0 * TB, b1 * TB)
                n = (b1 - b0) * TB
                iota = iota_e[:].unsqueeze(1).to_broadcast([P, n, E])
                wide = lambda a: a.unsqueeze(2).to_broadcast([P, n, E])
                if r == 0:
                    v.wait_ge(consts, 5 + E)
                v.wait_ge(lg_ready, b1)
                after(tick(nc.vector.tensor_copy(lg[:, s], tp[1][:, s.start * E:s.stop * E].rearrange("p (n e) -> p n e", e=E))))
                for j, src in enumerate((lg, lgm)):
                    after(tick(nc.vector.tensor_reduce(top[:, j, s], src[:, s], AX.X, ALU.max)))
                    after(tick(nc.vector.tensor_tensor(eq[:, s], src[:, s], wide(top[:, j, s]), ALU.is_equal)))
                    after(tick(nc.vector.scalar_tensor_tensor(out=cand[:, j, s], in0=eq[:, s], scalar=-float(E), in1=iota,
                                                              op0=ALU.mult, op1=ALU.add)))
                    after(tick(nc.vector.tensor_reduce(first[:, j, s], cand[:, j, s], AX.X, ALU.min)))
                    after(tick(nc.vector.tensor_tensor(oh[:, j, s], cand[:, j, s], wide(first[:, j, s]), ALU.is_equal)))
                    if j == 0:
                        after(tick(nc.vector.scalar_tensor_tensor(out=lgm[:, s], in0=oh[:, 0, s], scalar=-3e38, in1=lg[:, s],
                                                                  op0=ALU.mult, op1=ALU.add)))
                nc.vector.tensor_tensor(hot[:, s], oh[:, 0, s], oh[:, 1, s], ALU.add).then_inc(hot_ready, 1)
                nc.vector.tensor_tensor(dtop[:, s], top[:, 0, s], top[:, 1, s], ALU.subtract).then_inc(dtop_ready, 1)
                tick(nc.vector.tensor_scalar(eidx[:, :, s], first[:, :, s], float(E), None, ALU.add))

            def place(r):
                b0, b1 = ROUNDS[r]
                s = slice(b0 * TB, b1 * TB)
                v.wait_ge(pos_ready, r + 1)
                counts = tp[1][:, 64 + s.start * E:64 + s.stop * E].rearrange("p (n e) -> p n e", e=E)
                tick(nc.vector.tensor_tensor(ohp[:, 0, s], counts, oh[:, 0, s], ALU.mult))
                after(tick(nc.vector.tensor_tensor(ohp[:, 1, s], counts, oh[:, 1, s], ALU.mult)))
                after(tick(nc.vector.tensor_reduce(pos[:, :, s], ohp[:, :, s], AX.X, ALU.add)))
                tick(nc.vector.scalar_tensor_tensor(out=slot[:, :, s], in0=eidx[:, :, s], scalar=float(CAP), in1=pos[:, :, s],
                                                    op0=ALU.mult, op1=ALU.add))
                after(tick(nc.vector.tensor_scalar(over[:, :, s], pos[:, :, s], float(CAP), float(2 * SLOTS), ALU.is_ge, ALU.mult)))
                nc.vector.tensor_tensor(put_at[:, :, s], slot[:, :, s], over[:, :, s], ALU.add).then_inc(put_ready, 1)
                tick(nc.vector.tensor_scalar(posc[:, :, s], pos[:, :, s], float(CAP - 1), None, ALU.min))
                after(tick(nc.vector.tensor_scalar(valid[:, :, s], pos[:, :, s], float(CAP), None, ALU.is_lt)))
                tick(nc.vector.scalar_tensor_tensor(out=get_at[:, :, s], in0=eidx[:, :, s], scalar=float(CAP), in1=posc[:, :, s],
                                                    op0=ALU.mult, op1=ALU.add))
                v.wait_ge(dth_ready, r + 1)
                tick(nc.vector.tensor_scalar(cw[:, 0, s], dth[:, s], 0.5, 0.5, ALU.mult, ALU.add))
                after(tick(nc.vector.tensor_scalar(cw[:, 1, s], dth[:, s], -0.5, 0.5, ALU.mult, ALU.add)))
                nc.vector.tensor_tensor(cw[:, :, s], cw[:, :, s], valid[:, :, s], ALU.mult).then_inc(routed, 1)

            for step in range(6):
                wkv(0, 0, step)
            for b in range(B):
                for j in range(NCHUNK):
                    hidden(b * NCHUNK + j)
                    for r, (_, b1) in enumerate(ROUNDS):
                        if b == b1 - 1 and j == 0:
                            route(r)
                        if b == b1 - 1 and j == RANK_AT:
                            place(r)
                    if b + 1 < B:
                        wkv(0, b + 1, j)
                take_shared(b)
            steps = [(b, i) for b in range(B) for i in range(6)]
            for c in range(nshared, nchunks):
                done = (c - nshared) * len(steps) // (2 * E)
                upto = (c - nshared + 1) * len(steps) // (2 * E)
                hidden(c)
                for b, i in steps[done:upto]:
                    wkv(1, b, i)

            for b in range(B):
                v.wait_ge(gathered[b], 16 * 2 * TB)
                if b == 0:
                    v.wait_ge(routed, len(ROUNDS))
                    v.wait_ge(sh_taken, B)
                for i in range(TB):
                    n_ = b * TB + i
                    after(tick(nc.vector.scalar_tensor_tensor(out=xt[:, n_], in0=got_of(b, 0, i), scalar=cw[:, 0, n_:n_ + 1],
                                                              in1=xt[:, n_], op0=ALU.mult, op1=ALU.add)))
                    nc.vector.scalar_tensor_tensor(out=xt[:, n_], in0=got_of(b, 1, i), scalar=cw[:, 1, n_:n_ + 1],
                                                   in1=xt[:, n_], op0=ALU.mult, op1=ALU.add).then_inc(x1_ready, 1)
                v.wait_ge(tanh1_done, b + 1)
                nc.vector.scalar_tensor_tensor(out=h1[:, b % 2], in0=h1[:, b % 2], scalar=1.0, in1=euk[:, 1, b],
                                               op0=ALU.add, op1=ALU.mult).then_inc(h1_ready, 1)
                v.wait_ge(gate1_ready, b + 1)
                g = tp[1][:, 0:TB * E].rearrange("p (n e) -> p n e", e=E)
                for i in range(TB):
                    n = tick(nc.vector.max(top1[:, b, i], g[:, i]))
                after(n)
                nc.vector.tensor_tensor(dtop1[:, b], top1[:, b, :, 0], top1[:, b, :, 1], ALU.subtract).then_inc(dtop1_ready, 1)
                v.wait_ge(dth1_ready, b + 1)
                tick(nc.vector.tensor_scalar(rw[:, b, 0], dth1[:, b], 0.5, 0.5, ALU.mult, ALU.add))
                after(tick(nc.vector.tensor_scalar(rw[:, b, 1], dth1[:, b], -0.5, 0.5, ALU.mult, ALU.add)))
                after(tick(nc.vector.tensor_tensor(rw[:, b, 2], rw[:, b, 0], rw[:, b, 1], ALU.add)))
                for i in range(TB):
                    n_ = b * TB + i
                    v.wait_ge(y_ready, n_ + 1)
                    after(tick(nc.vector.scalar_tensor_tensor(out=xt[:, n_], in0=dn[i][:, C:2 * C], scalar=rw[:, b, 2, i:i + 1],
                                                              in1=xt[:, n_], op0=ALU.mult, op1=ALU.add)))
                    nc.vector.tensor_tensor(xt[:, n_], dn[i][:, 0:C], xt[:, n_], ALU.add).then_inc(y_done, 1)

        @block.tensor
        def _(pe):
            def mm(dst, w, m, first, last):
                return nc.tensor.matmul(dst, w, m, start=first, stop=last)

            pe.wait_ge(consts, 5 + E)
            for b in range(B):
                pe.wait_ge(h0_ready, b + 1)
                if b >= 1:
                    pe.wait_ge(htok_ready, b)
                for i in range(TB):
                    for c in range(CH):
                        last = nc.tensor.transpose(tp[0][:, i * C + c * P:i * C + (c + 1) * P], xc[:, b, c, i * P:(i + 1) * P], ident[:])
                last.then_inc(htp_ready, 1)
                if b == 0:
                    pe.wait_ge(ld_router, 16)
                for r, (b0, _) in enumerate(ROUNDS):
                    if b == b0 and r:
                        pe.wait_ge(put_ready, r)
                for i in range(TB):
                    n = b * TB + i
                    for c in range(CH):
                        last = mm(tp[1][:, n * E:(n + 1) * E], xc[:, b, c, i * P:(i + 1) * P], router_s[:, c], c == 0, c == CH - 1)
                last.then_inc(lg_ready, 1)
                for j in range(NCHUNK):
                    u = b * NCHUNK + j
                    if b == 0 and j % 2 == 0:
                        pe.wait_ge(ld_sup[j // 2], 16)
                    if chunk_before(u):
                        pe.wait_ge(hid_ready, chunk_before(u))
                    bank_ = hb[chunk_banks[u][0]]
                    for half in range(2 if j < JC else 1):
                        for c in range(CH):
                            wcols = 2 * P if j < JC else 2 * JR
                            at = j * CH * 2 * P + c * wcols + half * P
                            last = mm(bank_[:, half * T:half * T + T], sup_s[:, at:at + P], xc[:, b, c], c == 0, c == CH - 1)
                    last.then_inc(up_ready, 1)
                    for r, (b0, b1) in enumerate(ROUNDS):
                        if b == b1 - 1 and j == RANK_AT:
                            ranks(pe, mm, r)
                if b == 0:
                    pe.wait_ge(ld_sdn, 32)
                pe.wait_ge(hid_ready, (b + 1) * NCHUNK)
                if b >= 2:
                    pe.wait_ge(sh_taken, b - 1)
                for i in range(TB):
                    for j in range(NCHUNK):
                        rows = P if j < JC else JR
                        last = mm(dn[b % 2][:, i * C:(i + 1) * C], hid[0:rows, b % 2, j, i * P:(i + 1) * P], sdn_s[0:rows, j],
                                  j == 0, j == NCHUNK - 1)
                last.then_inc(sh_ready, 1)

            def slots_T(q):
                pe.wait_ge(ld_buf[q], 16)
                for i in range(3):
                    t = 3 * q + i
                    if t >= 2:
                        pe.wait_ge(bufT_ready, t - 1)
                    else:
                        pe.wait_ge(htok_ready, B)
                        pe.wait_ge(routed, len(ROUNDS))
                    n = min(2, 5 - 2 * i)
                    for c in range(CH):
                        for s in range(n):
                            at = (c * n + s) * P
                            last = nc.tensor.transpose(tp[t % 2][:, at:at + P], buf[:, q % 2, 2 * i + s, c * P:(c + 1) * P], ident[:])
                    last.then_inc(btp_ready, 1)

            def expert_up(e):
                if e % 2 == 0:
                    pe.wait_ge(ld_mup[e // 2], 16)
                pe.wait_ge(bufT_ready, 3 * (e // 2) + 3)
                for j in range(2):
                    u = nshared + 2 * e + j
                    pe.wait_ge(hid_ready, chunk_before(u))
                    for half in range(2 - j):
                        at, m = (half * IA, IA) if j == 0 else (2 * IA, 2 * IB)
                        for c in range(CH):
                            last = mm(hb[chunk_banks[u][half]][0:m, 0:CAP], mup_s[:, e, c, at:at + m],
                                      bufT[:, (e // 2) % 2, c, (e % 2) * CAP:(e % 2 + 1) * CAP], c == 0, c == CH - 1)
                    last.then_inc(up_ready, 1)

            def expert_down(e):
                if e == 0:
                    pe.wait_ge(ld_mdn, 32)
                    pe.wait_ge(sh_taken, B)
                pe.wait_ge(hid_ready, nshared + 2 * e + 2)
                for r in range(3):
                    m = min(P, CAP - r * P)
                    if e >= 1 and r != 1:
                        pe.wait_ge(mo_taken, 2 * (e - 1) + (1 if r == 0 else 2))
                    for j, rows in enumerate((IA, IB)):
                        last = mm(dn[r // 2][0:m, (r % 2) * C:(r % 2 + 1) * C], hidm[0:rows, e % 2, j, r * P:r * P + m],
                                  mdn_s[0:rows, e, j], j == 0, j == 1)
                    if r >= 1:
                        last.then_inc(mo_ready, 1)

            slots_T(0)
            for e in range(E):
                expert_up(e)
                if e % 2 == 1 and e < E - 1:
                    slots_T((e + 1) // 2)
                if e >= 1:
                    expert_down(e - 1)
            expert_down(E - 1)

            pe.wait_ge(ld_l1, 32)
            pe.wait_ge(bufT_ready, 3 * (E // 2))
            pe.wait_ge(hid_ready, nchunks)
            pe.wait_ge(mo_taken, 2 * E)
            for b in range(B):
                for i in range(TB):
                    pe.wait_ge(x1_ready, b * TB + i + 1)
                    if b >= 1 and i == 0:
                        pe.wait_ge(tanh1_done, b)
                    for c in range(CH):
                        last = nc.tensor.transpose(tp[0][:, c * T + i * P:c * T + (i + 1) * P], xt[:, b * TB + i, c * P:(c + 1) * P], ident[:])
                last.then_inc(x1T_ready, 1)
                pe.wait_ge(h1_ready, b + 1)
                if b >= 1:
                    pe.wait_ge(dtop1_ready, b)
                for i in range(TB):
                    for c in range(CH):
                        last = mm(tp[1][:, i * E:(i + 1) * E], h1[:, b % 2, c, i * P:(i + 1) * P], l1g_s[:, c], c == 0, c == CH - 1)
                last.then_inc(gate1_ready, 1)
                if b >= 2:
                    pe.wait_ge(relu_done, b - 1)
                for o in range(CH):
                    for c in range(CH):
                        last = mm(hb[b % 2][:, o * T:(o + 1) * T], l1_s[:, 0, c, o * P:(o + 1) * P], h1[:, b % 2, c], c == 0, c == CH - 1)
                last.then_inc(up1_ready, 1)
                for i in range(TB):
                    if b >= 1:
                        pe.wait_ge(y_done, (b - 1) * TB + i + 1)
                    for c in range(CH):
                        mm(dn[i][:, C:2 * C], h1[:, b % 2, c, i * P:(i + 1) * P], l1_s[:, 2, c], c == 0, c == CH - 1)
                    pe.wait_ge(relu_done, b + 1)
                    for c in range(CH):
                        last = mm(dn[i][:, 0:C], hid1[:, b % 2, c, i * P:(i + 1) * P], l1_s[:, 1, c], c == 0, c == CH - 1)
                    last.then_inc(y_ready, 1)


def rev(a):
    return a[:, ::-1]


def _lay_out(x, fside_BxSxS_0, cond_512, L0_cond_w, L0_cond_u, L0_ffn_router, L0_ffn_w_up_gate, L0_ffn_w_down,
             L0_ffn_shared_w_up_gate, L0_ffn_shared_w_down, L1_cond_w, L1_cond_u, L1_ffn_W_up, L1_ffn_W_down,
             L1_ffn_W_gate, L1_ffn_W_expert):
    import numpy as np

    def channels(a):
        return a.transpose(2, 0, 1).reshape(CH, P, B, T).transpose(1, 2, 0, 3)

    def rows(w):
        return w.reshape(CH, P, -1).transpose(1, 0, 2)

    g, u = L0_ffn_shared_w_up_gate[:, :J], L0_ffn_shared_w_up_gate[:, J:]
    sup = [rows(np.concatenate([g[:, j * P:(j + 1) * P], u[:, j * P:(j + 1) * P]], 1)).reshape(P, -1) for j in range(JC)]
    sup.append(rows(np.concatenate([u[:, JC * P:], g[:, JC * P:]], 1)).reshape(P, -1))
    m = L0_ffn_w_up_gate
    mg, mu = m[:, :, :I], m[:, :, I:]
    mup = np.concatenate([mg[..., :IA], mu[..., :IA], mu[..., IA:], mg[..., IA:]], 2)
    return {
        "x_cm": channels(x),
        "x_tm": x.reshape(NT, P, C).transpose(1, 0, 2),
        "k_cm": channels(fside_BxSxS_0),
        "cond": cond_512,
        "wu": np.stack([L0_cond_w, L1_cond_w, L0_cond_u, L1_cond_u]).reshape(4, CH, P).transpose(2, 0, 1),
        "router": rows(L0_ffn_router),
        "sup": np.concatenate(sup, 1),
        "sdn": L0_ffn_shared_w_down,
        "mup": mup.reshape(E, CH, P, 2 * I).transpose(2, 0, 1, 3),
        "mdn": L0_ffn_w_down,
        "l1w": np.stack([rows(L1_ffn_W_up.T), rows(L1_ffn_W_down.T), rows(L1_ffn_W_expert)], 1),
        "l1g": rows(L1_ffn_W_gate.T),
    }


def kernel(**inputs):
    import numpy as np
    import concourse.bacc as bacc
    from concourse.bass_utils import run_bass_kernel_spmd

    arrays = {n: np.ascontiguousarray(a) for n, a in _lay_out(**{n: np.asarray(a) for n, a in inputs.items()}).items()}
    nc = bacc.Bacc("TRN2", target_bir_lowering=False, num_devices=1)
    args = {n: nc.dram_tensor(n, a.shape, F32, kind="ExternalInput").ap() for n, a in arrays.items()}
    out = nc.dram_tensor("out", (B * T, C), F32, kind="ExternalOutput").ap()
    adaln_ffn(nc, **args, out=out)
    r = run_bass_kernel_spmd(nc, [arrays], core_ids=[0])
    return r.results[0]["out"].reshape(B, T, C)
```

```python
from contextlib import ExitStack

import concourse.bass as bass
from concourse import mybir

F32 = mybir.dt.float32
BF16 = mybir.dt.bfloat16
U32 = mybir.dt.uint32
ALU = mybir.AluOpType
ACT = mybir.ActivationFunctionType
AX = mybir.AxisListType

P = 128
B, T, C = 4, 256, 256
CH = C // P
NT = B * T // P
TB = T // P
E, CAP = 8, 320
I, J = 176, 704
IA = 112
IB = I - IA
JC = J // P
JR = J - JC * P
SLOTS = E * CAP
EXP30 = 10686474581524.463
ROUNDS = ((0, 2), (2, 3), (3, 4))
NCHUNK = JC + 1
SPLIT = 4
TURN_AT = {1: 6, 2: 11, 3: 14}
ROUTE_AT = (7, 11, 14)
RANK_AT = (8, 12, 15)
STEPS0 = (2, 1, 1, 1, 2, 1, 3, 3, 1, 1, 1, 1, 1, 1, 1)
STEPS1 = (1, 1, 1, 1, 2, 1, 2, 1, 2, 1, 2, 1, 2, 1, 1, 0)
CAP1_AT = (12, 13, 14, 15)
DOWN_BEHIND = (7, 13, 19)
TAKE_BEHIND = (9, 15, 21)



def adaln_ffn(nc, x_cm, x_tm, k_cm, cond, wu, router, sup, sdn, mup, mdn, l1w, l1e, out):
    slots_in = nc.dram_tensor("slots_in", (SLOTS, C), F32).ap()
    slots_out = nc.dram_tensor("slots_out", (SLOTS, C), F32).ap()

    with ExitStack() as ctx:
        def sb(name, shape, dt=F32):
            return ctx.enter_context(nc.sbuf_tensor(name, shape, dt))

        def sem(name):
            return ctx.enter_context(nc.semaphore(name))

        def sems(name, n):
            return [sem(f"{name}{i}") for i in range(n)]

        k = sb("k", [P, B, CH, T])
        xc = sb("xc", [P, B, CH, T])
        xt = sb("xt", [P, NT, C])
        ek = sb("ek", [P, B, CH, T])
        ekv = sb("ekv", [P, B, CH, T])
        euk = sb("euk", [P, 2, B, CH, T])
        nf = sb("nf", [P, CH, T])
        nb = sb("nb", [P, CH, T + 1])
        df = sb("df", [P, CH, T])
        db = sb("db", [P, CH, T + 1])
        euv = sb("euv", [P, CH, T])
        rden = sb("rden", [P, CH, T])
        htok = sb("htok", [P, NT, C])
        wu_s = sb("wu_s", [P, 4, CH])
        cond_s = sb("cond_s", [P, B, 64])
        zsum = sb("zsum", [P, B])
        gate_t = sb("gate_t", [P, 3, B])
        halfp = sb("halfp", [P, B])
        oscale = sb("oscale", [P, B])
        noscale = sb("noscale", [P, B])
        ew = sb("ew", [P, 2, 2, CH])
        decay = sb("decay", [P, 2, B, CH])
        turn = sb("turn", [P, CH, P + E])
        sup_s = sb("sup_s", [P, CH * 2 * J])
        sdn_s = sb("sdn_s", [P, NCHUNK, C])
        mup_s = sb("mup_s", [P, E, CH, 2 * I])
        mdn_s = sb("mdn_s", [IA, E, 2, C])
        l1_s = sb("l1_s", [P, 2, CH, C])
        l1e_s = sb("l1e_s", [P, CH, C + E])
        ident = sb("ident", [P, P])
        before = sb("before", [P, P], BF16)
        ones = sb("ones", [P, P], BF16)
        iota_e = sb("iota_e", [P, E])
        zero = sb("zero", [P, 512])
        gate_a = sb("gate_a", [P, 2, CAP])
        hid = sb("hid", [P, 2, NCHUNK, T])
        buf = sb("buf", [P, 2, 5, C])
        bufT = sb("bufT", [P, 2, CH, 2 * CAP])
        hidm = sb("hidm", [IA, 2, 2, CAP])
        outb = sb("outb", [P, 2, 3, C])
        got = ek[:].rearrange("p b c t -> p (b c t)").rearrange("p (k n d) -> p k n d", k=2, n=TB * 2)
        got2 = ekv[:].rearrange("p b c t -> p (b c t)").rearrange("p (k n d) -> p k n d", k=2, n=TB * 2)
        lg = sb("lg", [P, NT, E])
        top8 = sb("top8", [P, NT, 8])
        idx8 = sb("idx8", [P, NT, 8], U32)
        oh = sb("oh", [P, 2, NT, E])
        hot = sb("hot", [P, NT, E], BF16)
        ohp = sb("ohp", [P, 2, NT, E])
        eidx = sb("eidx", [P, 2, NT])
        pos = sb("pos", [P, 2, NT])
        posc = sb("posc", [P, 2, NT])
        over = sb("over", [P, 2, NT])
        slot = sb("slot", [P, 2, NT])
        valid = sb("valid", [P, 2, NT])
        put_at = sb("put_at", [P, 2, NT], U32)
        get_at = sb("get_at", [P, 2, NT], U32)
        dtop = sb("dtop", [P, NT])
        dth = sb("dth", [P, NT])
        cw = sb("cw", [P, 2, NT])
        h1 = sb("h1", [P, 2, CH, T])
        hid1 = sb("hid1", [P, 2, CH, T])
        top1 = sb("top1", [P, B, TB, 8])
        dtop1 = sb("dtop1", [P, B, TB])
        dth1 = sb("dth1", [P, B, TB])
        rw = sb("rw", [P, B, 3, TB])

        def bank(name):
            return ctx.enter_context(nc.psum_tensor(name, [P, 512], F32))

        hb = [bank(f"hb{i}") for i in range(4)]
        dn = [bank(f"dn{i}") for i in range(2)]
        tp = [bank(f"tp{i}") for i in range(2)]

        shared = [("shared", b, j) for b in range(B) for j in range(NCHUNK)]
        chunks = shared[:(B - 1) * NCHUNK + SPLIT]
        nearly = len(chunks)
        chunks += [("expert", e, j) for e in range(E) for j in range(2)]
        nlate = len(chunks)
        chunks += shared[nearly:]
        nchunks = len(chunks)
        chunk_banks, unit = [], 0
        for kind, _, j in chunks:
            n = 2 if kind == "expert" and j == 0 else 1
            chunk_banks.append([(unit + i) % 4 for i in range(n)])
            unit += n

        exp_order = [(0, 0), (0, 1), (0, 2), (1, 0), (0, 3), (1, 1), (1, 2), (1, 3)]
        exp_count, n_exp = {}, 2
        for l, b in exp_order:
            n_exp += CH + (l == 0) + ((l, b) == (0, 0))
            exp_count[l, b] = n_exp
        EXP0 = [exp_count[0, b] for b in range(B)]
        EXP1 = [exp_count[1, b] for b in range(B)]

        def chunk_before(c):
            need = 0
            for b_ in chunk_banks[c]:
                last = max((i for i in range(c) if b_ in chunk_banks[i]), default=-1)
                need = max(need, last + 1)
            return need

        ld_k, ld_x = sems("ld_k", B), sems("ld_x", B)
        ld_small, ld_cond, ld_router = sem("ld_small"), sem("ld_cond"), sem("ld_router")
        ld_sup, ld_sdn, ld_xt = sems("ld_sup", 3), sem("ld_sdn"), sem("ld_xt")
        ld_mup, ld_mdn = sems("ld_mup", 4), sem("ld_mdn")
        ld_l1 = sem("ld_l1")
        consts = sem("consts")
        zeroed = sem("zeroed")
        capped = sem("capped")
        prep = sem("prep")
        scan_ready = sem("scan_ready")
        exp_done = sem("exp_done")
        tanh_done = sem("tanh_done")
        vec = sem("vec")
        h0_ready = sem("h0_ready")
        htp_ready = sem("htp_ready")
        htok_ready = sem("htok_ready")
        lg_ready = sem("lg_ready")
        den_ready = sem("den_ready")
        ln_done = sem("ln_done")
        rec_ready = sem("rec_ready")
        hot_ready = sem("hot_ready")
        pos_ready = sem("pos_ready")
        dtop_ready = sem("dtop_ready")
        dth_ready = sem("dth_ready")
        put_ready = sem("put_ready")
        routed = sem("routed")
        up_ready = sem("up_ready")
        silu_ready = sem("silu_ready")
        hid_ready = sem("hid_ready")
        sh_ready = sem("sh_ready")
        sh_taken = sem("sh_taken")
        scattered = sem("scattered")
        ld_buf = sems("ld_buf", E // 2)
        btp_ready = sem("btp_ready")
        bufT_ready = sem("bufT_ready")
        mo_ready = sem("mo_ready")
        mo_taken = sem("mo_taken")
        written = sems("written", 2)
        q1_ready = sem("q1_ready")
        gathered = sems("gathered", B)
        x1_ready = sem("x1_ready")
        x1T_ready = sem("x1T_ready")
        tanh1_done = sem("tanh1_done")
        h1_ready = sem("h1_ready")
        up1_ready = sem("up1_ready")
        relu_done = sem("relu_done")
        ex_ready = sem("ex_ready")
        dtop1_ready = sem("dtop1_ready")
        dth1_ready = sem("dth1_ready")
        y_ready = sem("y_ready")
        y_done = sem("y_done")
        stored = sem("stored")

        block = ctx.enter_context(nc.Block())

        def got_of(b, j, i):
            g = got if b < 2 else got2
            return g[:, j, (b % 2) * TB + i]

        def store_expert(sp, e):
            sp.wait_ge(mo_taken, 2 * (e + 1))
            rows = slots_out[e * CAP:(e + 1) * CAP]
            sp.dma_start(rows[0:2 * P].rearrange("(r p) d -> p r d", p=P), outb[:, e % 2, 0:2]).then_inc(written[e % 2], 16)
            sp.dma_start(rows[2 * P:CAP], outb[0:CAP - 2 * P, e % 2, 2]).then_inc(written[e % 2], 16)

        def ranks(pe, mm, r):
            b0, b1 = ROUNDS[r]
            n0, n1 = b0 * TB, b1 * TB
            pe.wait_ge(hot_ready, r + 1)
            dst = tp[1][:, 64 + n0 * E:64 + n1 * E]
            last = mm(dst, before[:], hot[:, n0:n1], True, n1 == 1)
            for n in range(n1 - 1):
                lo = max(n + 1, n0)
                last = mm(tp[1][:, 64 + lo * E:64 + n1 * E], ones[:], hot[:, n:n + 1].to_broadcast([P, n1 - lo, E]), False, n == n1 - 2)
            last.then_inc(pos_ready, 1)

        @block.sync
        def _(sp):
            sp.dma_start(wu_s[:], wu).then_inc(ld_small, 16)
            sp.dma_start(k[:, 0], k_cm[:, 0]).then_inc(ld_k[0], 16)
            sp.dma_start(cond_s[:], cond.unsqueeze(0).to_broadcast([P, B, 64])).then_inc(ld_cond, 16)
            sp.dma_start(xc[:, 0], x_cm[:, 0]).then_inc(ld_x[0], 16)
            sp.dma_start(turn[:, 0, P:], router[:, 0]).then_inc(ld_router, 16)
            sp.dma_start(turn[:, 1, 0:E], router[:, 1]).then_inc(ld_router, 16)
            for b in range(1, B):
                sp.dma_start(k[:, b], k_cm[:, b]).then_inc(ld_k[b], 16)
            sp.dma_start(xc[:, 1], x_cm[:, 1]).then_inc(ld_x[1], 16)
            for i, (a, z) in enumerate(((0, 1024), (1024, 2048), (2048, 2 * CH * J))):
                sp.dma_start(sup_s[:, a:z], sup[:, a:z]).then_inc(ld_sup[i], 16)
            sp.dma_start(xc[:, 2], x_cm[:, 2]).then_inc(ld_x[2], 16)
            sp.dma_start(sdn_s[:, 0:JC], sdn[0:JC * P].rearrange("(j p) d -> p j d", p=P)).then_inc(ld_sdn, 16)
            sp.dma_start(sdn_s[0:JR, JC], sdn[JC * P:J]).then_inc(ld_sdn, 16)
            sp.dma_start(xc[:, 3], x_cm[:, 3]).then_inc(ld_x[3], 16)
            sp.dma_start(xt[:], x_tm).then_inc(ld_xt, 16)
            sp.wait_ge(consts, 1)
            for i in range(10):
                sp.dma_start(slots_in[i * 256:(i + 1) * 256].rearrange("(p r) d -> p (r d)", r=2),
                             zero[:]).then_inc(zeroed, 16)
            for i in range(4):
                sp.dma_start(mup_s[:, 2 * i:2 * i + 2], mup[:, 2 * i:2 * i + 2]).then_inc(ld_mup[i], 16)
                if i == 0:
                    sp.dma_start(mdn_s[:, :, 0], mdn[:, 0:IA].rearrange("e i d -> i e d")).then_inc(ld_mdn, 16)
                    sp.dma_start(mdn_s[0:IB, :, 1], mdn[:, IA:I].rearrange("e i d -> i e d")).then_inc(ld_mdn, 16)
            sp.dma_start(l1_s[:], l1w).then_inc(ld_l1, 16)
            sp.dma_start(l1e_s[:], l1e).then_inc(ld_l1, 16)
            sp.wait_ge(scattered, 16 * 2 * NT)
            def load_pair(q):
                if q >= 2:
                    sp.wait_ge(btp_ready, 3 * (q - 1))
                sp.dma_start(buf[:, q % 2], slots_in[q * 640:(q + 1) * 640].rearrange("(r p) d -> p r d", p=P)).then_inc(ld_buf[q], 16)

            load_pair(0)
            load_pair(1)
            for q in range(E // 2):
                if q + 2 < E // 2:
                    load_pair(q + 2)
                store_expert(sp, 2 * q)
                store_expert(sp, 2 * q + 1)
            for n in range(NT):
                sp.wait_ge(y_done, n + 1)
                sp.dma_start(out[n * P:(n + 1) * P], xt[:, n]).then_inc(stored, 16)
            sp.wait_ge(stored, 16 * NT)

        @block.gpsimd
        def _(pool):
            nc.gpsimd.memset(zero[:], 0.0).then_inc(consts, 1)
            nc.gpsimd.memset(ident[:], 0.0).then_inc(consts, 1)
            nc.gpsimd.memset(ones[:], 1.0).then_inc(consts, 1)
            for e in range(E):
                nc.gpsimd.memset(iota_e[:, e:e + 1], float(e)).then_inc(consts, 1)
            pool.wait_ge(consts, 3 + E)
            nc.gpsimd.affine_select(out=ident[:], in_=ident[:], compare_op=ALU.not_equal, fill=1.0, base=0,
                                    pattern=[[-1, P]], channel_multiplier=1).then_inc(consts, 1)
            for c in range(CH):
                eye = turn[:, c, c * E:c * E + P]
                nc.gpsimd.affine_select(out=eye, in_=zero[:, 0:P], compare_op=ALU.not_equal, fill=1.0, base=0,
                                        pattern=[[-1, P]], channel_multiplier=1).then_inc(consts, 1)
            nc.gpsimd.affine_select(out=before[:], in_=ones[:], compare_op=ALU.is_ge, fill=0.0, base=-1,
                                    pattern=[[1, P]], channel_multiplier=-1).then_inc(consts, 1)
            steps = [0]

            def made(ins):
                steps[0] += 1
                ins.then_inc(prep, 1)
                return steps[0]

            def sums(l, b):
                pool.wait_ge(scan_ready, 8 * (l * B + b) + 4)
                made(nc.gpsimd.tensor_tensor(df[:], euk[:, l, b], df[:], ALU.add))
                pool.wait_ge(scan_ready, 8 * (l * B + b) + 8)
                made(nc.gpsimd.tensor_tensor(nf[:], euv[:] if l == 0 else k[:, b], nf[:], ALU.add))

            for b in range(B):
                pool.wait_ge(capped, b + 1)
                made(nc.gpsimd.tensor_tensor(ekv[:, b], ek[:, b], k[:, b], ALU.mult))
                if steps[0] > 1:
                    pool.wait_ge(prep, steps[0] - 1)
                pool.wait_ge(prep, made(nc.gpsimd.tensor_tensor(euv[:], euk[:, 0, b], k[:, b], ALU.mult)))
                sums(0, b)
            pool.wait_ge(zeroed, 160)
            for r, (b0, b1) in enumerate(ROUNDS):
                pool.wait_ge(put_ready, r + 1)
                pool.wait_ge(htok_ready, b1 * TB)
                for n in range(b0 * TB, b1 * TB):
                    for j in range(2):
                        nc.gpsimd.indirect_dma_start(
                            out=slots_in, out_offset=bass.IndirectOffsetOnAxis(ap=put_at[:, j, n:n + 1], axis=0),
                            in_=htok[:, n], in_offset=None, bounds_check=SLOTS - 1, oob_is_err=False).then_inc(scattered, 16)
            for b in range(B):
                pool.wait_ge(capped, B + b + 1)
                pool.wait_ge(prep, made(nc.gpsimd.tensor_tensor(k[:, b], euk[:, 1, b], k[:, b], ALU.mult)))
                sums(1, b)
            pool.wait_ge(written[0], 32 * (E // 2))
            pool.wait_ge(written[1], 32 * (E // 2))
            pool.wait_ge(q1_ready, B)
            pool.wait_ge(routed, 1)
            for b in range(B):
                for i in range(TB):
                    for j in range(2):
                        nc.gpsimd.indirect_dma_start(
                            out=got_of(b, j, i), out_offset=None, in_=slots_out,
                            in_offset=bass.IndirectOffsetOnAxis(ap=get_at[:, j, b * TB + i:b * TB + i + 1], axis=0)).then_inc(gathered[b], 16)

        @block.scalar
        def _(act):
            act.wait_ge(ld_small, 16)
            nc.scalar.activation(ew[:, 0], wu_s[:, 0:2], ACT.Exp).then_inc(exp_done, 1)
            act.wait_ge(exp_done, 1)
            nc.scalar.activation(ew[:, 1], ew[:, 0], ACT.Exp, scale=-1.0).then_inc(exp_done, 1)
            def exps(l, b):
                if l == 0:
                    act.wait_ge(ld_k[b], 16)
                    nc.scalar.activation(ek[:, b], k[:, b], ACT.Exp).then_inc(exp_done, 1)
                for c in range(CH):
                    nc.scalar.activation(euk[:, l, b, c], k[:, b, c], ACT.Exp, bias=wu_s[:, 2 + l, c:c + 1]).then_inc(exp_done, 1)
                if (l, b) == (0, 0):
                    act.wait_ge(vec, 1)
                    nc.scalar.activation(gate_t[:, 0], zsum[:], ACT.Exp, scale=-1.0).then_inc(exp_done, 1)

            def guess0():
                act.wait_ge(den_ready, 1)
                nc.scalar.activation(rden[:], df[:], ACT.Ln).then_inc(ln_done, 1)
                act.wait_ge(ln_done, 1)
                nc.scalar.activation(rden[:], rden[:], ACT.Exp, scale=-1.0).then_inc(rec_ready, 1)

            def tanh_x(b):
                act.wait_ge(ld_x[b], 16)
                nc.scalar.activation(xc[:, b], xc[:, b], ACT.Tanh, scale=0.5).then_inc(tanh_done, 1)

            for l, b in exp_order[:4]:
                exps(l, b)
            guess0()
            for l, b in exp_order[4:]:
                exps(l, b)
            for b in range(B):
                tanh_x(b)

            def turned(b):
                act.wait_ge(htp_ready, b + 1)
                for i in range(TB):
                    rows = tp[i][:, 0:2 * (P + E)].rearrange("p (c d) -> p c d", d=P + E)[:, :, 0:P]
                    nc.scalar.copy(htok[:, b * TB + i].rearrange("p (c d) -> p c d", d=P), rows).then_inc(htok_ready, 1)
                for i in range(TB):
                    nc.scalar.copy(lg[:, b * TB + i], tp[i][:, P:P + E]).then_inc(lg_ready, 1)

            def silu(c):
                act.wait_ge(up_ready, c + 1)
                if c >= 2:
                    act.wait_ge(hid_ready, c - 1)
                bank0 = hb[chunk_banks[c][0]]
                kind, _, j = chunks[c]
                if kind == "shared":
                    if j < JC:
                        src, dst = bank0[:, 0:T], gate_a[:, c % 2, 0:T]
                    else:
                        src, dst = bank0[P - JR:P, 0:T], gate_a[0:JR, c % 2, 0:T]
                elif j == 0:
                    src, dst = bank0[0:IA, 0:CAP], gate_a[0:IA, c % 2]
                else:
                    src, dst = bank0[P - IB:P, 0:CAP], gate_a[0:IB, c % 2]
                nc.scalar.activation(dst, src, ACT.Silu).then_inc(silu_ready, 1)

            def take_bufT(q):
                for i in range(3):
                    act.wait_ge(btp_ready, 3 * q + i + 1)
                    n = min(2, 5 - 2 * i)
                    dst = bufT[:, q % 2, :, 2 * i * P:(2 * i + n) * P]
                    src = tp[(3 * q + i) % 2][:, 0:n * CH * P].rearrange("p (c s) -> p c s", c=CH)
                    nc.scalar.copy(dst, src).then_inc(bufT_ready, 1)

            def take_out(e):
                if e >= 2:
                    act.wait_ge(written[e % 2], 32 * (e // 2))
                act.wait_ge(mo_ready, 2 * e + 1)
                nc.scalar.copy(outb[:, e % 2, 0:2], dn[0][:].rearrange("p (r d) -> p r d", r=2)).then_inc(mo_taken, 1)
                act.wait_ge(mo_ready, 2 * e + 2)
                nc.scalar.copy(outb[0:CAP - 2 * P, e % 2, 2], dn[1][0:CAP - 2 * P, 0:C]).then_inc(mo_taken, 1)

            turned(0)
            for c in range(nearly):
                for b, at in TURN_AT.items():
                    if c == at:
                        turned(b)
                silu(c)
                for r, (b0, b1) in enumerate(ROUNDS):
                    if c == ROUTE_AT[r]:
                        act.wait_ge(dtop_ready, r + 1)
                        nc.scalar.activation(dth[:, b0 * TB:b1 * TB], dtop[:, b0 * TB:b1 * TB], ACT.Tanh, scale=0.5).then_inc(dth_ready, 1)
            take_bufT(0)
            for e in range(E):
                for j in range(2):
                    silu(nearly + 2 * e + j)
                if e % 2 == 1 and e < E - 1:
                    take_bufT((e + 1) // 2)
                if e >= 1:
                    take_out(e - 1)
            take_out(E - 1)
            for c in range(nlate, nchunks):
                silu(c)

            def tanh_x1(b):
                act.wait_ge(x1T_ready, b + 1)
                if b >= 2:
                    act.wait_ge(ex_ready, b - 1)
                nc.scalar.activation(h1[:, b % 2], tp[b % 2][:].rearrange("p (c t) -> p c t", c=CH), ACT.Tanh, scale=0.5).then_inc(tanh1_done, 1)

            tanh_x1(0)
            for b in range(B):
                act.wait_ge(up1_ready, b + 1)
                if b >= 2:
                    act.wait_ge(y_ready, TB * (b - 1))
                nc.scalar.activation(hid1[:, b % 2], hb[b % 2][:].rearrange("p (c t) -> p c t", c=CH), ACT.Relu).then_inc(relu_done, 1)
                if b + 1 < B:
                    tanh_x1(b + 1)
                act.wait_ge(dtop1_ready, b + 1)
                nc.scalar.activation(dth1[:, b], dtop1[:, b], ACT.Tanh, scale=0.5).then_inc(dth1_ready, 1)

        @block.vector
        def _(v):
            ticks = [0]

            def tick(ins):
                ticks[0] += 1
                ins.then_inc(vec, 1)
                return ticks[0]

            def after(n):
                v.wait_ge(vec, n)

            v.wait_ge(ld_cond, 16)
            tick(nc.vector.reduce_sum(zsum[:], cond_s[:], AX.X))
            tick(nc.vector.memset(nb[:, :, T:T + 1], 0.0))
            tick(nc.vector.memset(db[:, :, T:T + 1], 0.0))
            v.wait_ge(exp_done, exp_count[0, 0])
            after(tick(nc.vector.tensor_scalar(gate_t[:, 1], gate_t[:, 0], 1.0, None, ALU.add)))
            after(tick(nc.vector.reciprocal(gate_t[:, 2], gate_t[:, 1])))
            tick(nc.vector.tensor_scalar(halfp[:], gate_t[:, 2], 0.5, 0.5, ALU.mult, ALU.add))
            tick(nc.vector.tensor_scalar(oscale[:], gate_t[:, 2], 0.1, 0.4, ALU.mult, ALU.add))
            after(tick(nc.vector.tensor_scalar(noscale[:], gate_t[:, 2], -0.1, -0.4, ALU.mult, ALU.add)))
            for l in range(2):
                for b in range(B):
                    n = tick(nc.vector.tensor_scalar(decay[:, l, b], ew[:, 1, l], halfp[:, b:b + 1], None, ALU.mult))
            after(n)

            def scans(src, fwd, bwd, dec, b):
                for c in range(CH):
                    d = dec[c].to_broadcast([P, T])
                    nc.vector.tensor_tensor_scan(fwd[:, c], d, src[:, b, c], 0.0, ALU.mult, ALU.add).then_inc(scan_ready, 1)
                    nc.vector.tensor_tensor_scan(rev(bwd[:, c, 0:T]), d, rev(src[:, b, c]), 0.0, ALU.mult, ALU.add).then_inc(scan_ready, 1)

            def both_ways(out, fwd, bwd, dec):
                for c in range(CH):
                    n = tick(nc.vector.scalar_tensor_tensor(out=out[:, c], in0=bwd[:, c, 1:T + 1], scalar=dec[c],
                                                            in1=fwd[:, c], op0=ALU.mult, op1=ALU.add))
                after(n)

            def cap(l, b):
                if l == 0:
                    v.wait_ge(exp_done, EXP0[b])
                    tick(nc.vector.tensor_scalar(ek[:, b], ek[:, b], EXP30, None, ALU.min))
                else:
                    v.wait_ge(exp_done, EXP1[b])
                nc.vector.tensor_scalar(euk[:, l, b], euk[:, l, b], EXP30, None, ALU.min).then_inc(capped, 1)
                v.wait_ge(capped, l * B + b + 1)

            def newton(den, r0):
                after(tick(nc.vector.tensor_tensor(den, den, r0, ALU.mult)))
                after(tick(nc.vector.scalar_tensor_tensor(out=den, in0=den, scalar=-2.0, in1=r0, op0=ALU.add, op1=ALU.mult)))

            def wkv(l, b, step):
                eu = euk[:, l, b]
                dec = [decay[:, l, b, c:c + 1] for c in range(CH)]
                den, num = (df[:], nf[:]) if l == 0 else (ek[:, b], ekv[:, b])
                den_sum = 4 * b + 3 if l == 0 else 4 * B + 3 * b + 2
                if step == 0:
                    if l == 0 and b == 0:
                        cap(0, 0)
                    scans(ek, df, db, dec, b)
                    if l == 0 and b + 1 < B:
                        cap(0, b + 1)
                elif step == 1:
                    if l == 0:
                        v.wait_ge(prep, den_sum - 2)
                    scans(ekv, nf, nb, dec, b)
                elif step == 2:
                    v.wait_ge(prep, den_sum)
                    both_ways(df, df, db, dec)
                    nc.vector.tensor_scalar(den, df[:], 1e-8, None, ALU.max).then_inc(den_ready, 1)
                elif step == 3:
                    v.wait_ge(prep, den_sum + 1)
                    both_ways(num, nf, nb, dec)
                    if l == 0 and b == 0:
                        v.wait_ge(rec_ready, 1)
                        newton(den, rden[:])
                elif step < 6:
                    if l == 1 or b > 0:
                        v.wait_ge(den_ready, l * B + b + 1)
                        half = den[:, step - 4]
                        after(tick(nc.vector.reciprocal(half, half)))
                elif l == 0:
                    scale = noscale if b == 0 else oscale
                    after(tick(nc.vector.scalar_tensor_tensor(out=nf[:], in0=nf[:], scalar=scale[:, b:b + 1],
                                                              in1=df[:], op0=ALU.mult, op1=ALU.mult)))
                    v.wait_ge(tanh_done, b + 1)
                    nc.vector.scalar_tensor_tensor(out=xc[:, b], in0=xc[:, b], scalar=1.0, in1=nf[:],
                                                   op0=ALU.add, op1=ALU.mult).then_inc(h0_ready, 1)
                    v.wait_ge(h0_ready, b + 1)
                else:
                    nc.vector.scalar_tensor_tensor(out=eu, in0=num, scalar=oscale[:, b:b + 1],
                                                   in1=den, op0=ALU.mult, op1=ALU.mult).then_inc(q1_ready, 1)
                    v.wait_ge(q1_ready, b + 1)

            def hidden(c):
                v.wait_ge(silu_ready, c + 1)
                banks = [hb[i] for i in chunk_banks[c]]
                kind, b, j = chunks[c]
                if kind == "shared":
                    if b >= 2:
                        v.wait_ge(sh_ready, b - 1)
                    if j < JC:
                        up, g, dst = banks[0][:, T:2 * T], gate_a[:, c % 2, 0:T], hid[:, b % 2, j]
                    else:
                        up, g, dst = banks[0][0:JR, 0:T], gate_a[0:JR, c % 2, 0:T], hid[0:JR, b % 2, j]
                else:
                    e = b
                    if e >= 2:
                        v.wait_ge(mo_ready, 2 * (e - 1))
                    if j == 0:
                        up, g, dst = banks[1][0:IA, 0:CAP], gate_a[0:IA, c % 2], hidm[:, e % 2, 0]
                    else:
                        up, g, dst = banks[0][0:IB, 0:CAP], gate_a[0:IB, c % 2], hidm[0:IB, e % 2, 1]
                nc.vector.tensor_tensor(dst, up, g, ALU.mult).then_inc(hid_ready, 1)

            def take_shared(b):
                v.wait_ge(sh_ready, b + 1)
                if b == 0:
                    v.wait_ge(ld_xt, 16)
                t = xt[:, b * TB:(b + 1) * TB]
                nc.vector.tensor_tensor(t, dn[b % 2][:].rearrange("p (n d) -> p n d", n=TB), t, ALU.add).then_inc(sh_taken, 1)

            def route(r):
                b0, b1 = ROUNDS[r]
                s = slice(b0 * TB, b1 * TB)
                n = (b1 - b0) * TB
                if r == 0:
                    v.wait_ge(consts, 7 + E)
                for i in range(s.start, s.stop):
                    v.wait_ge(lg_ready, i + 1)
                    last = tick(nc.vector.max(top8[:, i], lg[:, i]))
                after(last)
                for i in range(s.start, s.stop):
                    last = tick(nc.vector.max_index(idx8[:, i], top8[:, i], lg[:, i]))
                nc.vector.tensor_tensor(dtop[:, s], top8[:, s, 0], top8[:, s, 1], ALU.subtract).then_inc(dtop_ready, 1)
                after(last)
                after(tick(nc.vector.tensor_copy(eidx[:, :, s], idx8[:, s, 0:2].rearrange("p n j -> p j n"))))
                iota = iota_e[:].unsqueeze(1).to_broadcast([P, n, E])
                for j in range(2):
                    last = tick(nc.vector.tensor_tensor(oh[:, j, s], eidx[:, j, s].unsqueeze(2).to_broadcast([P, n, E]), iota, ALU.is_equal))
                after(last)
                nc.vector.tensor_tensor(hot[:, s], oh[:, 0, s], oh[:, 1, s], ALU.add).then_inc(hot_ready, 1)

            def place(r):
                b0, b1 = ROUNDS[r]
                s = slice(b0 * TB, b1 * TB)
                v.wait_ge(pos_ready, r + 1)
                counts = tp[0][:, s.start * E:s.stop * E].rearrange("p (n e) -> p n e", e=E)
                for j in range(2):
                    last = tick(nc.vector.tensor_tensor(ohp[:, j, s], counts, oh[:, j, s], ALU.mult))
                after(last)
                after(tick(nc.vector.tensor_reduce(pos[:, :, s], ohp[:, :, s], AX.X, ALU.add)))
                tick(nc.vector.scalar_tensor_tensor(out=slot[:, :, s], in0=eidx[:, :, s], scalar=float(CAP), in1=pos[:, :, s],
                                                    op0=ALU.mult, op1=ALU.add))
                after(tick(nc.vector.tensor_scalar(over[:, :, s], pos[:, :, s], float(CAP), float(2 * SLOTS), ALU.is_ge, ALU.mult)))
                nc.vector.tensor_tensor(put_at[:, :, s], slot[:, :, s], over[:, :, s], ALU.add).then_inc(put_ready, 1)

            def fetch():
                tick(nc.vector.tensor_scalar(posc[:], pos[:], float(CAP - 1), None, ALU.min))
                after(tick(nc.vector.tensor_scalar(valid[:], pos[:], float(CAP), None, ALU.is_lt)))
                tick(nc.vector.scalar_tensor_tensor(out=get_at[:], in0=eidx[:], scalar=float(CAP), in1=posc[:],
                                                    op0=ALU.mult, op1=ALU.add))
                v.wait_ge(dth_ready, len(ROUNDS))
                tick(nc.vector.tensor_scalar(cw[:, 0], dth[:], 0.5, 0.5, ALU.mult, ALU.add))
                after(tick(nc.vector.tensor_scalar(cw[:, 1], dth[:], -0.5, 0.5, ALU.mult, ALU.add)))
                nc.vector.tensor_tensor(cw[:], cw[:], valid[:], ALU.mult).then_inc(routed, 1)

            for step in range(7):
                wkv(0, 0, step)
            steps0 = [(0, b, i) for b in range(1, B) for i in range(7)]
            steps1 = [(1, b, i) for b in range(B) for i in range(7)]
            for c in range(nearly):
                for _ in range(STEPS0[c] if c < len(STEPS0) else 0):
                    wkv(*steps0.pop(0))
                hidden(c)
                for r in range(len(ROUNDS)):
                    if c == ROUTE_AT[r]:
                        route(r)
                    if c == RANK_AT[r]:
                        place(r)
                    if c == RANK_AT[r] + 1 and r == len(ROUNDS) - 1:
                        fetch()
                if c in CAP1_AT:
                    cap(1, CAP1_AT.index(c))
                if c > RANK_AT[-1]:
                    wkv(*steps1.pop(0))
                if c in TAKE_BEHIND:
                    take_shared(TAKE_BEHIND.index(c))
            for c in range(nearly, nlate):
                hidden(c)
                for _ in range(STEPS1[c - nearly]):
                    wkv(*steps1.pop(0))
            while steps1:
                wkv(*steps1.pop(0))
            for c in range(nlate, nchunks):
                hidden(c)

            def combine(b):
                v.wait_ge(gathered[b], 16 * 2 * TB)
                if b == 0:
                    v.wait_ge(routed, 1)
                v.wait_ge(sh_taken, b + 1)
                for i in range(TB):
                    n_ = b * TB + i
                    n = tick(nc.vector.scalar_tensor_tensor(out=xt[:, n_], in0=got_of(b, 0, i), scalar=cw[:, 0, n_:n_ + 1],
                                                            in1=xt[:, n_], op0=ALU.mult, op1=ALU.add))
                after(n)
                for i in range(TB):
                    n_ = b * TB + i
                    nc.vector.scalar_tensor_tensor(out=xt[:, n_], in0=got_of(b, 1, i), scalar=cw[:, 1, n_:n_ + 1],
                                                   in1=xt[:, n_], op0=ALU.mult, op1=ALU.add).then_inc(x1_ready, 1)

            def gate_x1(b):
                v.wait_ge(tanh1_done, b + 1)
                nc.vector.scalar_tensor_tensor(out=h1[:, b % 2], in0=h1[:, b % 2], scalar=1.0, in1=euk[:, 1, b],
                                               op0=ALU.add, op1=ALU.mult).then_inc(h1_ready, 1)

            take_shared(B - 1)
            combine(0)
            gate_x1(0)
            combine(1)
            for b in range(B):
                if b + 1 < B:
                    gate_x1(b + 1)
                v.wait_ge(ex_ready, b + 1)
                for i in range(TB):
                    n = tick(nc.vector.max(top1[:, b, i], hb[2 + i][:, C:C + E]))
                after(n)
                nc.vector.tensor_tensor(dtop1[:, b], top1[:, b, :, 0], top1[:, b, :, 1], ALU.subtract).then_inc(dtop1_ready, 1)
                if b + 2 < B:
                    combine(b + 2)
                v.wait_ge(dth1_ready, b + 1)
                tick(nc.vector.tensor_scalar(rw[:, b, 0], dth1[:, b], 0.5, 0.5, ALU.mult, ALU.add))
                after(tick(nc.vector.tensor_scalar(rw[:, b, 1], dth1[:, b], -0.5, 0.5, ALU.mult, ALU.add)))
                after(tick(nc.vector.tensor_tensor(rw[:, b, 2], rw[:, b, 0], rw[:, b, 1], ALU.add)))
                for i in range(TB):
                    n_ = b * TB + i
                    v.wait_ge(x1_ready, n_ + 1)
                    n = tick(nc.vector.scalar_tensor_tensor(out=xt[:, n_], in0=hb[2 + i][:, 0:C], scalar=rw[:, b, 2, i:i + 1],
                                                            in1=xt[:, n_], op0=ALU.mult, op1=ALU.add))
                after(n)
                for i in range(TB):
                    n_ = b * TB + i
                    v.wait_ge(y_ready, n_ + 1)
                    nc.vector.tensor_tensor(xt[:, n_], dn[i][:, 0:C], xt[:, n_], ALU.add).then_inc(y_done, 1)

        @block.tensor
        def _(pe):
            def mm(dst, w, m, first, last):
                return nc.tensor.matmul(dst, w, m, start=first, stop=last)

            def turn_rows(b):
                pe.wait_ge(h0_ready, b + 1)
                if b >= 1:
                    pe.wait_ge(lg_ready, b * TB)
                for r in range(1, len(ROUNDS)):
                    if b == ROUNDS[r][0]:
                        pe.wait_ge(put_ready, r)
                for i in range(TB):
                    for c in range(CH):
                        at = c * P
                        last = nc.tensor.matmul(tp[i][:, at:at + P + E], xc[:, b, c, i * P:(i + 1) * P], turn[:, c],
                                                start=c == 0, stop=c == CH - 1, skip_group_check=True)
                last.then_inc(htp_ready, 1)

            def shared_up(u):
                _, b, j = chunks[u]
                if b == 0 and j % 2 == 0:
                    pe.wait_ge(ld_sup[j // 2], 16)
                if chunk_before(u):
                    pe.wait_ge(hid_ready, chunk_before(u))
                bank_ = hb[chunk_banks[u][0]]
                for half in range(2 if j < JC else 1):
                    for c in range(CH):
                        wcols = 2 * P if j < JC else 2 * JR
                        at = j * CH * 2 * P + c * wcols + half * P
                        last = mm(bank_[:, half * T:half * T + T], sup_s[:, at:at + P], xc[:, b, c], c == 0, c == CH - 1)
                last.then_inc(up_ready, 1)

            def shared_down(b):
                if b == 0:
                    pe.wait_ge(ld_sdn, 32)
                pe.wait_ge(hid_ready, (b + 1) * NCHUNK if b < B - 1 else nchunks)
                if b >= 2:
                    pe.wait_ge(sh_taken, b - 1)
                if b == B - 1:
                    pe.wait_ge(mo_taken, 2 * E)
                for i in range(TB):
                    for j in range(NCHUNK):
                        rows = P if j < JC else JR
                        last = mm(dn[b % 2][:, i * C:(i + 1) * C], hid[0:rows, b % 2, j, i * P:(i + 1) * P], sdn_s[0:rows, j],
                                  j == 0, j == NCHUNK - 1)
                last.then_inc(sh_ready, 1)

            def ranks(r):
                b0, b1 = ROUNDS[r]
                n0, n1 = b0 * TB, b1 * TB
                pe.wait_ge(hot_ready, r + 1)
                pe.wait_ge(lg_ready, b1 * TB)
                mm(tp[0][:, n0 * E:n1 * E], before[:], hot[:, n0:n1], True, n1 == 1)
                for n in range(n1 - 1):
                    lo = max(n + 1, n0)
                    last = mm(tp[0][:, lo * E:n1 * E], ones[:], hot[:, n:n + 1].to_broadcast([P, n1 - lo, E]), False, n == n1 - 2)
                last.then_inc(pos_ready, 1)

            pe.wait_ge(consts, 7 + E)
            pe.wait_ge(ld_router, 32)
            turn_rows(0)
            for u in range(nearly):
                for b, at in TURN_AT.items():
                    if u == at:
                        turn_rows(b)
                shared_up(u)
                for r in range(len(ROUNDS)):
                    if u == RANK_AT[r]:
                        ranks(r)
                if u in DOWN_BEHIND:
                    shared_down(DOWN_BEHIND.index(u))

            def slots_T(q):
                pe.wait_ge(ld_buf[q], 16)
                for i in range(3):
                    t = 3 * q + i
                    if t >= 2:
                        pe.wait_ge(bufT_ready, t - 1)
                    else:
                        pe.wait_ge(put_ready, len(ROUNDS))
                    n = min(2, 5 - 2 * i)
                    for c in range(CH):
                        for s in range(n):
                            at = (c * n + s) * P
                            last = nc.tensor.transpose(tp[t % 2][:, at:at + P], buf[:, q % 2, 2 * i + s, c * P:(c + 1) * P], ident[:])
                    last.then_inc(btp_ready, 1)

            def expert_up(e):
                if e % 2 == 0:
                    pe.wait_ge(ld_mup[e // 2], 16)
                pe.wait_ge(bufT_ready, 3 * (e // 2) + 3)
                for j in range(2):
                    u = nearly + 2 * e + j
                    pe.wait_ge(hid_ready, chunk_before(u))
                    for half in range(2 - j):
                        at, m = (half * IA, IA) if j == 0 else (2 * IA, 2 * IB)
                        for c in range(CH):
                            last = mm(hb[chunk_banks[u][half]][0:m, 0:CAP], mup_s[:, e, c, at:at + m],
                                      bufT[:, (e // 2) % 2, c, (e % 2) * CAP:(e % 2 + 1) * CAP], c == 0, c == CH - 1)
                    last.then_inc(up_ready, 1)

            def expert_down(e):
                if e == 0:
                    pe.wait_ge(ld_mdn, 32)
                    pe.wait_ge(sh_taken, B - 1)
                pe.wait_ge(hid_ready, nearly + 2 * e + 2)
                for r in range(3):
                    m = min(P, CAP - r * P)
                    if e >= 1 and r != 1:
                        pe.wait_ge(mo_taken, 2 * (e - 1) + (1 if r == 0 else 2))
                    for j, rows in enumerate((IA, IB)):
                        last = mm(dn[r // 2][0:m, (r % 2) * C:(r % 2 + 1) * C], hidm[0:rows, e % 2, j, r * P:r * P + m],
                                  mdn_s[0:rows, e, j], j == 0, j == 1)
                    if r >= 1:
                        last.then_inc(mo_ready, 1)

            slots_T(0)
            for e in range(E):
                expert_up(e)
                if e % 2 == 1 and e < E - 1:
                    slots_T((e + 1) // 2)
                if e >= 1:
                    expert_down(e - 1)
            expert_down(E - 1)

            for u in range(nlate, nchunks):
                shared_up(u)
            shared_down(B - 1)

            def turn_x1(b):
                if b >= 2:
                    pe.wait_ge(tanh1_done, b - 1)
                for i in range(TB):
                    pe.wait_ge(x1_ready, b * TB + i + 1)
                    for c in range(CH):
                        last = nc.tensor.transpose(tp[b % 2][:, c * T + i * P:c * T + (i + 1) * P], xt[:, b * TB + i, c * P:(c + 1) * P], ident[:])
                last.then_inc(x1T_ready, 1)

            pe.wait_ge(ld_l1, 32)
            pe.wait_ge(bufT_ready, 3 * (E // 2))
            turn_x1(0)
            for b in range(B):
                pe.wait_ge(h1_ready, b + 1)
                if b >= 2:
                    pe.wait_ge(relu_done, b - 1)
                for o in range(CH):
                    for c in range(CH):
                        last = mm(hb[b % 2][:, o * T:(o + 1) * T], l1_s[:, 0, c, o * P:(o + 1) * P], h1[:, b % 2, c], c == 0, c == CH - 1)
                last.then_inc(up1_ready, 1)
                if b + 1 < B:
                    turn_x1(b + 1)
                if b >= 1:
                    pe.wait_ge(y_done, b * TB)
                else:
                    pe.wait_ge(sh_taken, B)
                for i in range(TB):
                    for c in range(CH):
                        last = mm(hb[2 + i][:, 0:C + E], h1[:, b % 2, c, i * P:(i + 1) * P], l1e_s[:, c], c == 0, c == CH - 1)
                last.then_inc(ex_ready, 1)
                pe.wait_ge(relu_done, b + 1)
                for i in range(TB):
                    for c in range(CH):
                        last = mm(dn[i][:, 0:C], hid1[:, b % 2, c, i * P:(i + 1) * P], l1_s[:, 1, c], c == 0, c == CH - 1)
                    last.then_inc(y_ready, 1)


def rev(a):
    return a[:, ::-1]


def _lay_out(x, fside_BxSxS_0, cond_512, L0_cond_w, L0_cond_u, L0_ffn_router, L0_ffn_w_up_gate, L0_ffn_w_down,
             L0_ffn_shared_w_up_gate, L0_ffn_shared_w_down, L1_cond_w, L1_cond_u, L1_ffn_W_up, L1_ffn_W_down,
             L1_ffn_W_gate, L1_ffn_W_expert):
    import numpy as np

    def channels(a):
        return a.transpose(2, 0, 1).reshape(CH, P, B, T).transpose(1, 2, 0, 3)

    def rows(w):
        return w.reshape(CH, P, -1).transpose(1, 0, 2)

    g, u = L0_ffn_shared_w_up_gate[:, :J], L0_ffn_shared_w_up_gate[:, J:]
    sup = [rows(np.concatenate([g[:, j * P:(j + 1) * P], u[:, j * P:(j + 1) * P]], 1)).reshape(P, -1) for j in range(JC)]
    sup.append(rows(np.concatenate([u[:, JC * P:], g[:, JC * P:]], 1)).reshape(P, -1))
    m = L0_ffn_w_up_gate
    mg, mu = m[:, :, :I], m[:, :, I:]
    mup = np.concatenate([mg[..., :IA], mu[..., :IA], mu[..., IA:], mg[..., IA:]], 2)
    return {
        "x_cm": channels(x),
        "x_tm": x.reshape(NT, P, C).transpose(1, 0, 2),
        "k_cm": channels(fside_BxSxS_0),
        "cond": cond_512,
        "wu": np.stack([L0_cond_w, L1_cond_w, L0_cond_u, L1_cond_u]).reshape(4, CH, P).transpose(2, 0, 1),
        "router": rows(L0_ffn_router),
        "sup": np.concatenate(sup, 1),
        "sdn": L0_ffn_shared_w_down,
        "mup": mup.reshape(E, CH, P, 2 * I).transpose(2, 0, 1, 3),
        "mdn": L0_ffn_w_down,
        "l1w": np.stack([rows(L1_ffn_W_up.T), rows(L1_ffn_W_down.T)], 1),
        "l1e": rows(np.concatenate([L1_ffn_W_expert, L1_ffn_W_gate.T], 1)),
    }


def kernel(**inputs):
    import numpy as np
    import concourse.bacc as bacc
    from concourse.bass_utils import run_bass_kernel_spmd

    arrays = {n: np.ascontiguousarray(a) for n, a in _lay_out(**{n: np.asarray(a) for n, a in inputs.items()}).items()}
    nc = bacc.Bacc("TRN2", target_bir_lowering=False, num_devices=1)
    args = {n: nc.dram_tensor(n, a.shape, F32, kind="ExternalInput").ap() for n, a in arrays.items()}
    out = nc.dram_tensor("out", (B * T, C), F32, kind="ExternalOutput").ap()
    adaln_ffn(nc, **args, out=out)
    r = run_bass_kernel_spmd(nc, [arrays], core_ids=[0])
    return r.results[0]["out"].reshape(B, T, C)
```

```python
from contextlib import ExitStack

import concourse.bass as bass
from concourse import mybir

F32 = mybir.dt.float32
F32R = mybir.dt.float32r
BF16 = mybir.dt.bfloat16
U32 = mybir.dt.uint32
ALU = mybir.AluOpType
ACT = mybir.ActivationFunctionType
AX = mybir.AxisListType

P = 128
B, T, C = 4, 256, 256
CH = C // P
NT = B * T // P
TB = T // P
E, CAP = 8, 320
I, J = 176, 704
IA = 112
IB = I - IA
JC = J // P
JR = J - JC * P
SLOTS = E * CAP
EXP30 = 10686474581524.463
ROUNDS = ((0, 2), (2, 3), (3, 4))
NCHUNK = JC + 1
L1W = CH * (3 * C + E)
SPLIT = 1
TURN_AT = {1: 6, 2: 11, 3: 14}
ROUTE_AT = (7, 12, 14)
RANK_AT = (8, 13, 14)
STEPS0 = (5, 1, 1, 1, 0, 2, 3, 1, 1, 1, 1, 1, 1, 2, 0)
STEPS1 = (0, 0, 1, 1, 1, 1, 1, 1, 1, 2, 1, 2, 1, 2, 1, 2, 1, 2, 1, 1, 0)
WEIGHTS_AT = (9, 10)
CAP1_AT = (14, 15, 16, 17)
DOWN_BEHIND = (7, 13, 18)
TAKE_BEHIND = (14, 16)

def adaln_ffn(nc, x_cm, x_tm, k_cm, cond, wu, router, sup, sdn, mup, mdn, l1w, out):
    slots_in = nc.dram_tensor("slots_in", (SLOTS, C), F32).ap()
    slots_out = nc.dram_tensor("slots_out", (SLOTS, C), F32).ap()

    with ExitStack() as ctx:
        def sb(name, shape, dt=F32):
            return ctx.enter_context(nc.sbuf_tensor(name, shape, dt))

        def sem(name):
            return ctx.enter_context(nc.semaphore(name))

        def sems(name, n):
            return [sem(f"{name}{i}") for i in range(n)]

        k = sb("k", [P, B, CH, T])
        xc = sb("xc", [P, B, CH, T])
        xt = sb("xt", [P, NT, C])
        ek = sb("ek", [P, B, CH, T])
        ekv = sb("ekv", [P, B, CH, T])
        euk = sb("euk", [P, 2, B, CH, T])
        nf = sb("nf", [P, CH, T])
        nb = sb("nb", [P, CH, T + 1])
        df = sb("df", [P, CH, T])
        db = sb("db", [P, CH, T + 1])
        euv = sb("euv", [P, CH, T])
        htok = sb("htok", [P, NT, C])
        wu_s = sb("wu_s", [P, 4, CH])
        cond_s = sb("cond_s", [P, B, 64])
        zsum = sb("zsum", [P, B])
        gate_t = sb("gate_t", [P, 3, B])
        halfp = sb("halfp", [P, B])
        oscale = sb("oscale", [P, B])
        ew = sb("ew", [P, 2, 2, CH])
        decay = sb("decay", [P, 2, B, CH])
        turn = sb("turn", [P, CH, P + E])
        sup_s = sb("sup_s", [P, CH * 2 * J])
        sdn_s = sb("sdn_s", [P, NCHUNK, C])
        mup_s = sb("mup_s", [P, 2, 2, CH, 2 * I])
        mup_w = sb("mup_w", [P, 2, 2, CH, 2 * I], F32R)
        mdn_s = sb("mdn_s", [IA, E, 2, C])
        l1_w = sb("l1_w", [P, 2, L1W], F32R)
        ident = sb("ident", [P, P])
        before = sb("before", [P, P], BF16)
        ones = sb("ones", [P, P], BF16)
        iota_e = sb("iota_e", [P, E])
        gate_a = sb("gate_a", [P, 2, CAP])
        hid = sb("hid", [P, 2, NCHUNK, T])
        buf = sb("buf", [P, 2, 5, C])
        bufT = sb("bufT", [P, 2, 2, CH, 2 * CAP], F32R)
        hidm = sb("hidm", [IA, 2, 2, CAP])
        outb = sb("outb", [P, 2, 3, C])
        zero = outb[:].rearrange("p k r d -> p (k r d)")[:, 0:512]
        got = ek[:].rearrange("p b c t -> p (b c t)").rearrange("p (k n d) -> p k n d", k=2, n=TB * 2)
        got2 = ekv[:].rearrange("p b c t -> p (b c t)").rearrange("p (k n d) -> p k n d", k=2, n=TB * 2)
        h1 = hid[:, 0, 0:2 * CH].rearrange("p (k c) t -> p k c t", k=2)
        l1_s = htok[:].rearrange("p n d -> p (n d)")[:, 0:L1W]
        h1_w, hid1_w = (bufT[:].rearrange("p k q c s -> p (k q c s)")[:, i * 4 * CH * T:(i + 1) * 4 * CH * T]
                        .rearrange("p (k q c t) -> p k q c t", k=2, q=2, c=CH) for i in range(2))
        lg = sb("lg", [P, NT, E])
        top8 = sb("top8", [P, NT, 8])
        idx8 = sb("idx8", [P, NT, 8], U32)
        eidx = sb("eidx", [P, 2, NT])
        oh = sb("oh", [P, 2, NT, E])
        hot = sb("hot", [P, NT, E], BF16)
        ohp = sb("ohp", [P, 2, NT, E])
        pos = sb("pos", [P, 2, NT])
        posc = sb("posc", [P, 2, NT])
        over = sb("over", [P, 2, NT])
        slot = sb("slot", [P, 2, NT])
        valid = sb("valid", [P, 2, NT])
        put_at = sb("put_at", [P, 2, NT], U32)
        get_at = sb("get_at", [P, 2, NT], U32)
        dtop = sb("dtop", [P, NT])
        dth = sb("dth", [P, NT])
        cw = sb("cw", [P, 2, NT])
        top1 = sb("top1", [P, B, TB, 8])
        dtop1 = sb("dtop1", [P, B, TB])
        dth1 = sb("dth1", [P, B, TB])
        rw = sb("rw", [P, B, 3, TB])

        def bank(name):
            return ctx.enter_context(nc.psum_tensor(name, [P, 512], F32))

        hb = [bank(f"hb{i}") for i in range(4)]
        dn = [bank(f"dn{i}") for i in range(2)]
        tp = [bank(f"tp{i}") for i in range(2)]

        shared = [("shared", b, j) for b in range(B) for j in range(NCHUNK)]
        chunks = shared[:(B - 1) * NCHUNK + SPLIT]
        nearly = len(chunks)
        chunks += [("expert", e, j) for e in range(E) for j in range(2)]
        nlate = len(chunks)
        chunks += shared[nearly:]
        nchunks = len(chunks)
        chunk_banks, unit = [], 0
        for kind, _, j in chunks:
            n = 2 if kind == "expert" and j == 0 else 1
            chunk_banks.append([(unit + i) % 4 for i in range(n)])
            unit += n

        steps1 = [(b, i) for b in range(B) for i in range(7)]
        plan1 = []
        for c in range(nlate):
            n = STEPS1[c - ROUTE_AT[-1]] if c >= ROUTE_AT[-1] else 0
            plan1.append([steps1.pop(0) for _ in range(n)])
        plan1.append(steps1)

        exp_order = [(0, 0), (0, 1), (0, 2), (0, 3), (1, 0), (1, 1), (1, 2), (1, 3)]
        exp_count, n_exp = {}, 3
        for l, b in exp_order:
            n_exp += CH + (l == 0)
            exp_count[l, b] = n_exp
        EXP0 = [exp_count[0, b] for b in range(B)]
        EXP1 = [exp_count[1, b] for b in range(B)]

        def chunk_before(c):
            need = 0
            for b_ in chunk_banks[c]:
                last = max((i for i in range(c) if b_ in chunk_banks[i]), default=-1)
                need = max(need, last + 1)
            return need

        ld_k, ld_x = sems("ld_k", B), sems("ld_x", B)
        ld_small, ld_cond, ld_router = sem("ld_small"), sem("ld_cond"), sem("ld_router")
        ld_sup, ld_sdn, ld_xt = sems("ld_sup", 3), sem("ld_sdn"), sem("ld_xt")
        ld_mup, ld_mdn = sems("ld_mup", E // 2), sem("ld_mdn")
        mup_hi = sem("mup_hi")
        mup_ready = sem("mup_ready")
        ld_l1 = sem("ld_l1")
        consts = sem("consts")
        zeroed = sem("zeroed")
        ek_capped = sem("ek_capped")
        capped = sem("capped")
        prep = sem("prep")
        scan_ready = sem("scan_ready")
        exp_done = sem("exp_done")
        tanh_done = sem("tanh_done")
        vec = sem("vec")
        h0_ready = sem("h0_ready")
        htp_ready = sem("htp_ready")
        htok_ready = sem("htok_ready")
        lg_ready = sem("lg_ready")
        den_ready = sem("den_ready")
        hot_ready = sem("hot_ready")
        pos_ready = sem("pos_ready")
        dtop_ready = sem("dtop_ready")
        dth_ready = sem("dth_ready")
        put_ready = sem("put_ready")
        routed = sem("routed")
        up_ready = sem("up_ready")
        silu_ready = sem("silu_ready")
        hid_ready = sem("hid_ready")
        sh_ready = sem("sh_ready")
        sh_taken = sem("sh_taken")
        scattered = sem("scattered")
        ld_head = sems("ld_head", E // 2)
        ld_buf = sems("ld_buf", E // 2)
        btp_ready = sem("btp_ready")
        bufT_hi = sem("bufT_hi")
        bufT_ready = sem("bufT_ready")
        mo_ready = sem("mo_ready")
        mo_taken = sem("mo_taken")
        written = sems("written", 2)
        q1_ready = sem("q1_ready")
        gathered = sems("gathered", B)
        x1_ready = sem("x1_ready")
        x1T_ready = sem("x1T_ready")
        tanh1_done = sem("tanh1_done")
        l1_hi, l1_ready = sem("l1_hi"), sem("l1_ready")
        h1_gated = sem("h1_gated")
        h1_hi = sem("h1_hi")
        h1_ready = sem("h1_ready")
        up1_ready = sem("up1_ready")
        relu_done = sem("relu_done")
        hid1_ready = sem("hid1_ready")
        ex_ready = sem("ex_ready")
        dtop1_ready = sem("dtop1_ready")
        dth1_ready = sem("dth1_ready")
        rw_ready = sem("rw_ready")
        ex_taken = sem("ex_taken")
        ex_added = sem("ex_added")
        y_ready = sem("y_ready")
        y_done = sem("y_done")
        stored = sem("stored")

        block = ctx.enter_context(nc.Block())

        def got_of(b, j, i):
            g = got if b < 2 else got2
            return g[:, j, (b % 2) * TB + i]

        def store_expert(sp, e):
            sp.wait_ge(mo_taken, 2 * (e + 1))
            rows = slots_out[e * CAP:(e + 1) * CAP]
            sp.dma_start(rows[0:2 * P].rearrange("(r p) d -> p r d", p=P), outb[:, e % 2, 0:2]).then_inc(written[e % 2], 16)
            sp.dma_start(rows[2 * P:CAP], outb[0:CAP - 2 * P, e % 2, 2]).then_inc(written[e % 2], 16)

        @block.sync
        def _(sp):
            sp.dma_start(wu_s[:], wu).then_inc(ld_small, 16)
            sp.dma_start(cond_s[:], cond.unsqueeze(0).to_broadcast([P, B, 64])).then_inc(ld_cond, 16)
            sp.dma_start(k[:, 0], k_cm[:, 0]).then_inc(ld_k[0], 16)
            sp.dma_start(xc[:, 0], x_cm[:, 0]).then_inc(ld_x[0], 16)
            sp.dma_start(turn[:, 0, P:], router[:, 0]).then_inc(ld_router, 16)
            sp.dma_start(turn[:, 1, 0:E], router[:, 1]).then_inc(ld_router, 16)
            for b in range(1, B):
                sp.dma_start(k[:, b], k_cm[:, b]).then_inc(ld_k[b], 16)
            sp.dma_start(xc[:, 1], x_cm[:, 1]).then_inc(ld_x[1], 16)
            for i, (a, z) in enumerate(((0, 1024), (1024, 2048), (2048, 2 * CH * J))):
                sp.dma_start(sup_s[:, a:z], sup[:, a:z]).then_inc(ld_sup[i], 16)
            sp.dma_start(xc[:, 2], x_cm[:, 2]).then_inc(ld_x[2], 16)
            sp.dma_start(sdn_s[:, 0:JC], sdn[0:JC * P].rearrange("(j p) d -> p j d", p=P)).then_inc(ld_sdn, 16)
            sp.dma_start(sdn_s[0:JR, JC], sdn[JC * P:J]).then_inc(ld_sdn, 16)
            sp.dma_start(xc[:, 3], x_cm[:, 3]).then_inc(ld_x[3], 16)
            sp.dma_start(xt[:], x_tm).then_inc(ld_xt, 16)
            sp.wait_ge(consts, 1)
            for i in range(10):
                sp.dma_start(slots_in[i * 256:(i + 1) * 256].rearrange("(p r) d -> p (r d)", r=2),
                             zero).then_inc(zeroed, 16)

            def load_mup(q):
                if q >= 2:
                    sp.wait_ge(mup_ready, 2 * (q - 1))
                sp.dma_start(mup_s[:, q % 2], mup[:, 2 * q:2 * q + 2]).then_inc(ld_mup[q], 16)

            load_mup(0)
            sp.dma_start(mdn_s[:, :, 0], mdn[:, 0:IA].rearrange("e i d -> i e d")).then_inc(ld_mdn, 16)
            sp.dma_start(mdn_s[0:IB, :, 1], mdn[:, IA:I].rearrange("e i d -> i e d")).then_inc(ld_mdn, 16)
            load_mup(1)

            def load_pair(q):
                if q >= 2:
                    sp.wait_ge(btp_ready, 3 * (q - 1))
                rows = slots_in[q * 2 * CAP:(q + 1) * 2 * CAP].rearrange("(r p) d -> p r d", p=P)
                sp.dma_start(buf[:, q % 2, 0:2], rows[:, 0:2]).then_inc(ld_head[q], 16)
                sp.dma_start(buf[:, q % 2, 2:], rows[:, 2:]).then_inc(ld_buf[q], 16)

            sp.wait_ge(scattered, 16 * 2 * NT)
            load_pair(0)
            load_pair(1)
            sp.dma_start(l1_s, l1w).then_inc(ld_l1, 16)
            for q in range(E // 2):
                if q + 2 < E // 2:
                    load_pair(q + 2)
                    load_mup(q + 2)
                store_expert(sp, 2 * q)
                store_expert(sp, 2 * q + 1)
            for n in range(NT):
                sp.wait_ge(y_done, n + 1)
                sp.dma_start(out[n * P:(n + 1) * P], xt[:, n]).then_inc(stored, 16)
            sp.wait_ge(stored, 16 * NT)

        @block.gpsimd
        def _(pool):
            nc.gpsimd.memset(zero, 0.0).then_inc(consts, 1)
            nc.gpsimd.memset(ident[:], 0.0).then_inc(consts, 1)
            nc.gpsimd.memset(ones[:], 1.0).then_inc(consts, 1)
            for e in range(E):
                nc.gpsimd.memset(iota_e[:, e:e + 1], float(e)).then_inc(consts, 1)
            pool.wait_ge(consts, 3 + E)
            nc.gpsimd.affine_select(out=ident[:], in_=ident[:], compare_op=ALU.not_equal, fill=1.0, base=0,
                                    pattern=[[-1, P]], channel_multiplier=1).then_inc(consts, 1)
            for c in range(CH):
                eye = turn[:, c, c * E:c * E + P]
                nc.gpsimd.affine_select(out=eye, in_=zero[:, 0:P], compare_op=ALU.not_equal, fill=1.0, base=0,
                                        pattern=[[-1, P]], channel_multiplier=1).then_inc(consts, 1)
            nc.gpsimd.affine_select(out=before[:], in_=ones[:], compare_op=ALU.is_ge, fill=0.0, base=-1,
                                    pattern=[[1, P]], channel_multiplier=-1).then_inc(consts, 1)
            steps = [0]

            def made(ins):
                steps[0] += 1
                ins.then_inc(prep, 1)
                return steps[0]

            def add_den(l, b):
                pool.wait_ge(scan_ready, 8 * (l * B + b) + 4)
                made(nc.gpsimd.tensor_tensor(df[:], euk[:, l, b], df[:], ALU.add))

            def add_num(l, b):
                pool.wait_ge(scan_ready, 8 * (l * B + b) + 8)
                made(nc.gpsimd.tensor_tensor(nf[:], euv[:] if l == 0 else k[:, b], nf[:], ALU.add))

            for b in range(B):
                pool.wait_ge(ek_capped, b + 1)
                made(nc.gpsimd.tensor_tensor(ekv[:, b], ek[:, b], k[:, b], ALU.mult))
                if steps[0] > 1:
                    pool.wait_ge(prep, steps[0] - 1)
                pool.wait_ge(capped, b + 1)
                pool.wait_ge(prep, made(nc.gpsimd.tensor_tensor(euv[:], euk[:, 0, b], k[:, b], ALU.mult)))
                add_den(0, b)
                add_num(0, b)
            def split_mup(e):
                pool.wait_ge(mup_hi, e + 1)
                nc.gpsimd.tensor_tensor(mup_w[:, e % 2, 1], mup_s[:, (e // 2) % 2, e % 2], mup_w[:, e % 2, 0].bitcast(F32),
                                        ALU.subtract).then_inc(mup_ready, 1)

            pool.wait_ge(zeroed, 160)
            for r, (b0, b1) in enumerate(ROUNDS):
                if r == 1:
                    split_mup(0)
                    split_mup(1)
                pool.wait_ge(put_ready, r + 1)
                pool.wait_ge(htok_ready, b1 * TB)
                for n in range(b0 * TB, b1 * TB):
                    for j in range(2):
                        nc.gpsimd.indirect_dma_start(
                            out=slots_in, out_offset=bass.IndirectOffsetOnAxis(ap=put_at[:, j, n:n + 1], axis=0),
                            in_=htok[:, n], in_offset=None, bounds_check=SLOTS - 1, oob_is_err=False).then_inc(scattered, 16)

            def help1(c):
                for b, step in plan1[c]:
                    if step == 0:
                        pool.wait_ge(capped, B + b + 1)
                        pool.wait_ge(prep, made(nc.gpsimd.tensor_tensor(k[:, b], euk[:, 1, b], k[:, b], ALU.mult)))
                        add_den(1, b)
                    elif step == 1:
                        add_num(1, b)

            for c in range(nearly):
                help1(c)
            for e in range(E):
                help1(nearly + 2 * e)
                if e + 2 < E:
                    split_mup(e + 2)
                if e >= E - 2:
                    half = slice((e - E + 2) * L1W // 2, (e - E + 3) * L1W // 2)
                    pool.wait_ge(l1_hi, e - E + 3)
                    nc.gpsimd.tensor_tensor(l1_w[:, 1, half], l1_s[:, half], l1_w[:, 0, half].bitcast(F32), ALU.subtract).then_inc(l1_ready, 1)
                help1(nearly + 2 * e + 1)
            help1(nlate)
            pool.wait_ge(written[0], 32 * (E // 2))
            pool.wait_ge(written[1], 32 * (E // 2))
            pool.wait_ge(q1_ready, B)
            pool.wait_ge(routed, 1)
            for b in range(B):
                for i in range(TB):
                    for j in range(2):
                        nc.gpsimd.indirect_dma_start(
                            out=got_of(b, j, i), out_offset=None, in_=slots_out,
                            in_offset=bass.IndirectOffsetOnAxis(ap=get_at[:, j, b * TB + i:b * TB + i + 1], axis=0)).then_inc(gathered[b], 16)
            for b in range(1, B - 1):
                pool.wait_ge(h1_hi, CH * (b + 2))
                nc.gpsimd.tensor_tensor(h1_w[:, (b + 1) % 2, 1, 1], h1[:, (b + 1) % 2, 1], h1_w[:, (b + 1) % 2, 0, 1].bitcast(F32),
                                        ALU.subtract).then_inc(h1_ready, 1)
                for i in range(TB):
                    n = b * TB + i
                    pool.wait_ge(ex_taken, n + 1)
                    nc.gpsimd.tensor_tensor(xt[:, n], euv[:, i], xt[:, n], ALU.add).then_inc(ex_added, 1)

        @block.scalar
        def _(act):
            act.wait_ge(ld_small, 16)
            nc.scalar.activation(ew[:, 0], wu_s[:, 0:2], ACT.Exp).then_inc(exp_done, 1)
            act.wait_ge(exp_done, 1)
            nc.scalar.activation(ew[:, 1], ew[:, 0], ACT.Exp, scale=-1.0).then_inc(exp_done, 1)
            act.wait_ge(vec, 1)
            nc.scalar.activation(gate_t[:, 0], zsum[:], ACT.Exp, scale=-1.0).then_inc(exp_done, 1)

            def exps(l, b):
                if l == 0:
                    act.wait_ge(ld_k[b], 16)
                    nc.scalar.activation(ek[:, b], k[:, b], ACT.Exp).then_inc(exp_done, 1)
                for c in range(CH):
                    nc.scalar.activation(euk[:, l, b, c], k[:, b, c], ACT.Exp, bias=wu_s[:, 2 + l, c:c + 1]).then_inc(exp_done, 1)

            def tanh_x(b):
                act.wait_ge(ld_x[b], 16)
                nc.scalar.activation(xc[:, b], xc[:, b], ACT.Tanh, scale=0.5).then_inc(tanh_done, 1)

            for l, b in exp_order[:3]:
                exps(l, b)
            for b in range(2):
                tanh_x(b)
            for l, b in exp_order[3:]:
                exps(l, b)
            for b in range(2, B):
                tanh_x(b)

            def turned(b):
                act.wait_ge(htp_ready, b + 1)
                for i in range(TB):
                    rows = tp[i][:, 0:2 * (P + E)].rearrange("p (c d) -> p c d", d=P + E)[:, :, 0:P]
                    nc.scalar.copy(htok[:, b * TB + i].rearrange("p (c d) -> p c d", d=P), rows).then_inc(htok_ready, 1)
                for i in range(TB):
                    nc.scalar.copy(lg[:, b * TB + i], tp[i][:, P:P + E]).then_inc(lg_ready, 1)

            def silu(c):
                act.wait_ge(up_ready, c + 1)
                if c >= 2:
                    act.wait_ge(hid_ready, c - 1)
                bank0 = hb[chunk_banks[c][0]]
                kind, _, j = chunks[c]
                if kind == "shared":
                    if j < JC:
                        src, dst = bank0[:, 0:T], gate_a[:, c % 2, 0:T]
                    else:
                        src, dst = bank0[P - JR:P, 0:T], gate_a[0:JR, c % 2, 0:T]
                elif j == 0:
                    src, dst = bank0[0:IA, 0:CAP], gate_a[0:IA, c % 2]
                else:
                    src, dst = bank0[P - IB:P, 0:CAP], gate_a[0:IB, c % 2]
                nc.scalar.activation(dst, src, ACT.Silu).then_inc(silu_ready, 1)

            def take_bufT(t):
                q, i = divmod(t, 3)
                act.wait_ge(btp_ready, t + 1)
                n = min(2, 5 - 2 * i)
                dst = bufT[:, q % 2, 0, :, 2 * i * P:(2 * i + n) * P]
                src = tp[t % 2][:, 0:n * CH * P].rearrange("p (c s) -> p c s", c=CH)
                nc.scalar.copy(dst, src).then_inc(bufT_hi, 1)

            def high_mup(e):
                if e % 2 == 0:
                    act.wait_ge(ld_mup[e // 2], 16)
                if e >= 2:
                    act.wait_ge(up_ready, nearly + 2 * (e - 1))
                nc.scalar.copy(mup_w[:, e % 2, 0], mup_s[:, (e // 2) % 2, e % 2]).then_inc(mup_hi, 1)

            def take_out(e):
                if e >= 2:
                    act.wait_ge(written[e % 2], 32 * (e // 2))
                act.wait_ge(mo_ready, 2 * e + 1)
                nc.scalar.copy(outb[:, e % 2, 0:2], dn[0][:].rearrange("p (r d) -> p r d", r=2)).then_inc(mo_taken, 1)
                act.wait_ge(mo_ready, 2 * e + 2)
                nc.scalar.copy(outb[0:CAP - 2 * P, e % 2, 2], dn[1][0:CAP - 2 * P, 0:C]).then_inc(mo_taken, 1)

            turned(0)
            for c in range(nearly):
                for b, at in TURN_AT.items():
                    if c == at:
                        turned(b)
                silu(c)
                if c in WEIGHTS_AT:
                    high_mup(WEIGHTS_AT.index(c))
                for r, (b0, b1) in enumerate(ROUNDS):
                    if c == ROUTE_AT[r]:
                        act.wait_ge(dtop_ready, r + 1)
                        nc.scalar.activation(dth[:, b0 * TB:b1 * TB], dtop[:, b0 * TB:b1 * TB], ACT.Tanh, scale=0.5).then_inc(dth_ready, 1)
            for t in range(3):
                take_bufT(t)
            for e in range(E + 1):
                turned_pair = e % 2 == 0 and e + 2 < E
                t = 3 * (e // 2 + 1)
                if e < E:
                    silu(nearly + 2 * e)
                    silu(nearly + 2 * e + 1)
                if turned_pair:
                    take_bufT(t)
                    take_bufT(t + 1)
                if e % 2 == 1 and e + 1 < E:
                    take_bufT(3 * (e + 1) // 2 + 2)
                if e + 2 < E:
                    high_mup(e + 2)
                elif e < E:
                    half = slice((e - E + 2) * L1W // 2, (e - E + 3) * L1W // 2)
                    act.wait_ge(ld_l1, 16)
                    nc.scalar.copy(l1_w[:, 0, half], l1_s[:, half]).then_inc(l1_hi, 1)
                if e >= 1:
                    take_out(e - 1)
            for c in range(nlate, nchunks):
                silu(c)

            def tanh_x1(b):
                act.wait_ge(x1T_ready, b + 1)
                if b >= 2:
                    act.wait_ge(ex_ready, b - 1)
                nc.scalar.activation(h1[:, b % 2], tp[b % 2][:].rearrange("p (c t) -> p c t", c=CH), ACT.Tanh, scale=0.5).then_inc(tanh1_done, 1)

            def high_h1(b):
                for c in range(CH):
                    act.wait_ge(h1_gated, CH * b + c + 1)
                    nc.scalar.copy(h1_w[:, b % 2, 0, c], h1[:, b % 2, c]).then_inc(h1_hi, 1)

            tanh_x1(0)
            high_h1(0)
            for b in range(B):
                act.wait_ge(up1_ready, b + 1)
                if b >= 2:
                    act.wait_ge(y_ready, TB * (b - 1))
                nc.scalar.activation(hid1_w[:, b % 2, 0], hb[b % 2][:].rearrange("p (c t) -> p c t", c=CH), ACT.Relu).then_inc(relu_done, 1)
                if b + 1 < B:
                    tanh_x1(b + 1)
                    high_h1(b + 1)
                act.wait_ge(dtop1_ready, b + 1)
                nc.scalar.activation(dth1[:, b], dtop1[:, b], ACT.Tanh, scale=0.5).then_inc(dth1_ready, 1)
                if 1 <= b < B - 1:
                    act.wait_ge(rw_ready, b + 1)
                    for i in range(TB):
                        if b >= 2:
                            act.wait_ge(ex_added, (b - 2) * TB + i + 1)
                        nc.scalar.activation(euv[:, i], hb[2 + i][:, 0:C], ACT.Copy, scale=rw[:, b, 2, i:i + 1]).then_inc(ex_taken, 1)

        @block.vector
        def _(v):
            ticks = [0]

            def tick(ins):
                ticks[0] += 1
                ins.then_inc(vec, 1)
                return ticks[0]

            def after(n):
                v.wait_ge(vec, n)

            v.wait_ge(ld_cond, 16)
            tick(nc.vector.reduce_sum(zsum[:], cond_s[:], AX.X))
            tick(nc.vector.memset(nb[:, :, T:T + 1], 0.0))
            tick(nc.vector.memset(db[:, :, T:T + 1], 0.0))
            v.wait_ge(exp_done, 3)
            after(tick(nc.vector.tensor_scalar(gate_t[:, 1], gate_t[:, 0], 1.0, None, ALU.add)))
            after(tick(nc.vector.reciprocal(gate_t[:, 2], gate_t[:, 1])))
            after(tick(nc.vector.tensor_scalar(halfp[:], gate_t[:, 2], 0.5, 0.5, ALU.mult, ALU.add)))

            def decays(l, b):
                return tick(nc.vector.tensor_scalar(decay[:, l, b], ew[:, 1, l], halfp[:, b:b + 1], None, ALU.mult))

            after(decays(0, 0))

            def scans(src, fwd, bwd, dec, b):
                for c in range(CH):
                    d = dec[c].to_broadcast([P, T])
                    nc.vector.tensor_tensor_scan(fwd[:, c], d, src[:, b, c], 0.0, ALU.mult, ALU.add).then_inc(scan_ready, 1)
                    nc.vector.tensor_tensor_scan(rev(bwd[:, c, 0:T]), d, rev(src[:, b, c]), 0.0, ALU.mult, ALU.add).then_inc(scan_ready, 1)

            def both_ways(out, fwd, bwd, dec):
                for c in range(CH):
                    n = tick(nc.vector.scalar_tensor_tensor(out=out[:, c], in0=bwd[:, c, 1:T + 1], scalar=dec[c],
                                                            in1=fwd[:, c], op0=ALU.mult, op1=ALU.add))
                after(n)

            def cap_ek(b):
                v.wait_ge(exp_done, EXP0[b] - CH)
                nc.vector.tensor_scalar(ek[:, b], ek[:, b], EXP30, None, ALU.min).then_inc(ek_capped, 1)

            def cap_euk(l, b):
                v.wait_ge(exp_done, (EXP0, EXP1)[l][b])
                nc.vector.tensor_scalar(euk[:, l, b], euk[:, l, b], EXP30, None, ALU.min).then_inc(capped, 1)

            def wkv(l, b, step):
                eu = euk[:, l, b]
                dec = [decay[:, l, b, c:c + 1] for c in range(CH)]
                den, num = (df[:], nf[:]) if l == 0 else (ek[:, b], ekv[:, b])
                den_sum = 4 * b + 3 if l == 0 else 4 * B + 3 * b + 2
                if step == 0:
                    if l == 0 and b == 0:
                        cap_ek(0)
                    if l == 0:
                        v.wait_ge(ek_capped, b + 1)
                    scans(ek, df, db, dec, b)
                    if l == 0 and b == 0:
                        cap_euk(0, 0)
                elif step == 1:
                    if l == 0:
                        v.wait_ge(prep, den_sum - 2)
                    scans(ekv, nf, nb, dec, b)
                    if l == 0 and b + 1 < B:
                        cap_ek(b + 1)
                        cap_euk(0, b + 1)
                elif step == 2:
                    v.wait_ge(prep, den_sum)
                    both_ways(df, df, db, dec)
                    nc.vector.tensor_scalar(den, df[:], 1e-8, None, ALU.max).then_inc(den_ready, 1)
                elif step == 3:
                    v.wait_ge(prep, den_sum + 1)
                    both_ways(num, nf, nb, dec)
                elif step < 6:
                    v.wait_ge(den_ready, l * B + b + 1)
                    half = den[:, step - 4]
                    after(tick(nc.vector.reciprocal(half, half)))
                elif l == 0:
                    after(tick(nc.vector.scalar_tensor_tensor(out=nf[:], in0=nf[:], scalar=oscale[:, b:b + 1],
                                                              in1=df[:], op0=ALU.mult, op1=ALU.mult)))
                    v.wait_ge(tanh_done, b + 1)
                    nc.vector.scalar_tensor_tensor(out=xc[:, b], in0=xc[:, b], scalar=1.0, in1=nf[:],
                                                   op0=ALU.add, op1=ALU.mult).then_inc(h0_ready, 1)
                    v.wait_ge(h0_ready, b + 1)
                else:
                    nc.vector.scalar_tensor_tensor(out=eu, in0=num, scalar=oscale[:, b:b + 1],
                                                   in1=den, op0=ALU.mult, op1=ALU.mult).then_inc(q1_ready, 1)
                    v.wait_ge(q1_ready, b + 1)

            def hidden(c):
                v.wait_ge(silu_ready, c + 1)
                banks = [hb[i] for i in chunk_banks[c]]
                kind, b, j = chunks[c]
                if kind == "shared":
                    if b >= 2:
                        v.wait_ge(sh_ready, b - 1)
                    if j < JC:
                        up, g, dst = banks[0][:, T:2 * T], gate_a[:, c % 2, 0:T], hid[:, b % 2, j]
                    else:
                        up, g, dst = banks[0][0:JR, 0:T], gate_a[0:JR, c % 2, 0:T], hid[0:JR, b % 2, j]
                else:
                    e = b
                    if e >= 2:
                        v.wait_ge(mo_ready, 2 * (e - 1))
                    if j == 0:
                        up, g, dst = banks[1][0:IA, 0:CAP], gate_a[0:IA, c % 2], hidm[:, e % 2, 0]
                    else:
                        up, g, dst = banks[0][0:IB, 0:CAP], gate_a[0:IB, c % 2], hidm[0:IB, e % 2, 1]
                nc.vector.tensor_tensor(dst, up, g, ALU.mult).then_inc(hid_ready, 1)

            def split_bufT(t):
                q, i = divmod(t, 3)
                v.wait_ge(bufT_hi, t + 1)
                n = min(2, 5 - 2 * i)
                at = slice(2 * i * P, (2 * i + n) * P)
                src = tp[t % 2][:, 0:n * CH * P].rearrange("p (c s) -> p c s", c=CH)
                nc.vector.tensor_tensor(bufT[:, q % 2, 1, :, at], src, bufT[:, q % 2, 0, :, at].bitcast(F32),
                                        ALU.subtract).then_inc(bufT_ready, 1)

            def take_shared(b):
                v.wait_ge(sh_ready, b + 1)
                if b == 0:
                    v.wait_ge(ld_xt, 16)
                t = xt[:, b * TB:(b + 1) * TB]
                nc.vector.tensor_tensor(t, dn[b % 2][:].rearrange("p (n d) -> p n d", n=TB), t, ALU.add).then_inc(sh_taken, 1)

            def route(r):
                b0, b1 = ROUNDS[r]
                s = slice(b0 * TB, b1 * TB)
                n = (b1 - b0) * TB
                if r == 0:
                    v.wait_ge(consts, 7 + E)
                for i in range(s.start, s.stop):
                    v.wait_ge(lg_ready, i + 1)
                    last = tick(nc.vector.max(top8[:, i], lg[:, i]))
                after(last)
                for i in range(s.start, s.stop):
                    last = tick(nc.vector.max_index(idx8[:, i], top8[:, i], lg[:, i]))
                nc.vector.tensor_tensor(dtop[:, s], top8[:, s, 0], top8[:, s, 1], ALU.subtract).then_inc(dtop_ready, 1)
                after(last)
                after(tick(nc.vector.tensor_copy(eidx[:, :, s], idx8[:, s, 0:2].rearrange("p n j -> p j n"))))
                iota = iota_e[:].unsqueeze(1).to_broadcast([P, n, E])
                for j in range(2):
                    last = tick(nc.vector.tensor_tensor(oh[:, j, s], eidx[:, j, s].unsqueeze(2).to_broadcast([P, n, E]), iota, ALU.is_equal))
                after(last)
                nc.vector.tensor_tensor(hot[:, s], oh[:, 0, s], oh[:, 1, s], ALU.add).then_inc(hot_ready, 1)

            def place(r):
                b0, b1 = ROUNDS[r]
                s = slice(b0 * TB, b1 * TB)
                v.wait_ge(pos_ready, r + 1)
                counts = tp[0][:, s.start * E:s.stop * E].rearrange("p (n e) -> p n e", e=E)
                for j in range(2):
                    last = tick(nc.vector.tensor_tensor(ohp[:, j, s], counts, oh[:, j, s], ALU.mult))
                after(last)
                after(tick(nc.vector.tensor_reduce(pos[:, :, s], ohp[:, :, s], AX.X, ALU.add)))
                tick(nc.vector.scalar_tensor_tensor(out=slot[:, :, s], in0=eidx[:, :, s], scalar=float(CAP), in1=pos[:, :, s],
                                                    op0=ALU.mult, op1=ALU.add))
                after(tick(nc.vector.tensor_scalar(over[:, :, s], pos[:, :, s], float(CAP), float(2 * SLOTS), ALU.is_ge, ALU.mult)))
                nc.vector.tensor_tensor(put_at[:, :, s], slot[:, :, s], over[:, :, s], ALU.add).then_inc(put_ready, 1)

            def fetch():
                tick(nc.vector.tensor_scalar(posc[:], pos[:], float(CAP - 1), None, ALU.min))
                after(tick(nc.vector.tensor_scalar(valid[:], pos[:], float(CAP), None, ALU.is_lt)))
                tick(nc.vector.scalar_tensor_tensor(out=get_at[:], in0=eidx[:], scalar=float(CAP), in1=posc[:],
                                                    op0=ALU.mult, op1=ALU.add))
                v.wait_ge(dth_ready, len(ROUNDS))
                tick(nc.vector.tensor_scalar(cw[:, 0], dth[:], 0.5, 0.5, ALU.mult, ALU.add))
                after(tick(nc.vector.tensor_scalar(cw[:, 1], dth[:], -0.5, 0.5, ALU.mult, ALU.add)))
                nc.vector.tensor_tensor(cw[:], cw[:], valid[:], ALU.mult).then_inc(routed, 1)

            for step in range(7):
                wkv(0, 0, step)
                if step == 1:
                    tick(nc.vector.tensor_scalar(oscale[:], gate_t[:, 2], 0.1, 0.4, ALU.mult, ALU.add))
                    for b in range(1, B):
                        decays(0, b)
            steps0 = [(0, b, i) for b in range(1, B) for i in range(7)]
            for c in range(nearly):
                for _ in range(STEPS0[c] if c < len(STEPS0) else 0):
                    wkv(*steps0.pop(0))
                for r in range(len(ROUNDS)):
                    if c == ROUTE_AT[r]:
                        route(r)
                hidden(c)
                for r in range(len(ROUNDS)):
                    if c == RANK_AT[r]:
                        place(r)
                    if c == RANK_AT[r] + 1 and r == len(ROUNDS) - 1:
                        fetch()
                if c in CAP1_AT:
                    cap_euk(1, CAP1_AT.index(c))
                if c == ROUTE_AT[-1]:
                    for b in range(B):
                        decays(1, b)
                for b, step in plan1[c]:
                    wkv(1, b, step)
                if c in TAKE_BEHIND:
                    take_shared(TAKE_BEHIND.index(c))
            for t in range(3):
                split_bufT(t)
            take_shared(B - 2)
            for c in range(nearly, nlate):
                hidden(c)
                e, j = divmod(c - nearly, 2)
                turned_pair = e % 2 == 0 and e + 2 < E and j == 1
                t = 3 * (e // 2 + 1)
                if turned_pair:
                    split_bufT(t)
                    split_bufT(t + 1)
                if e % 2 == 1 and e + 1 < E and j == 1:
                    split_bufT(3 * (e + 1) // 2 + 2)
                for b, step in plan1[c]:
                    wkv(1, b, step)
            for b, step in plan1[nlate]:
                wkv(1, b, step)
            for c in range(nlate, nchunks):
                hidden(c)

            def combine(b):
                v.wait_ge(gathered[b], 16 * 2 * TB)
                if b == 0:
                    v.wait_ge(routed, 1)
                v.wait_ge(sh_taken, b + 1)
                for i in range(TB):
                    n_ = b * TB + i
                    n = tick(nc.vector.scalar_tensor_tensor(out=xt[:, n_], in0=got_of(b, 0, i), scalar=cw[:, 0, n_:n_ + 1],
                                                            in1=xt[:, n_], op0=ALU.mult, op1=ALU.add))
                after(n)
                for i in range(TB):
                    n_ = b * TB + i
                    nc.vector.scalar_tensor_tensor(out=xt[:, n_], in0=got_of(b, 1, i), scalar=cw[:, 1, n_:n_ + 1],
                                                   in1=xt[:, n_], op0=ALU.mult, op1=ALU.add).then_inc(x1_ready, 1)

            def gate_x1(b):
                v.wait_ge(tanh1_done, b + 1)
                for c in range(CH):
                    nc.vector.scalar_tensor_tensor(out=h1[:, b % 2, c], in0=h1[:, b % 2, c], scalar=1.0, in1=euk[:, 1, b, c],
                                                   op0=ALU.add, op1=ALU.mult).then_inc(h1_gated, 1)

            def low_h1(b):
                for c in range(CH if b < 2 else 1):
                    v.wait_ge(h1_hi, CH * b + c + 1)
                    nc.vector.tensor_tensor(h1_w[:, b % 2, 1, c], h1[:, b % 2, c], h1_w[:, b % 2, 0, c].bitcast(F32),
                                            ALU.subtract).then_inc(h1_ready, 1)

            combine(0)
            gate_x1(0)
            low_h1(0)
            combine(1)
            take_shared(B - 1)
            for b in range(B):
                v.wait_ge(relu_done, b + 1)
                nc.vector.scalar_tensor_tensor(out=hid1_w[:, b % 2, 1], in0=hb[b % 2][:].rearrange("p (c t) -> p c t", c=CH), scalar=0.0,
                                               in1=hid1_w[:, b % 2, 0].bitcast(F32), op0=ALU.max, op1=ALU.subtract).then_inc(hid1_ready, 1)
                if b + 1 < B:
                    gate_x1(b + 1)
                v.wait_ge(ex_ready, b + 1)
                for i in range(TB):
                    n = tick(nc.vector.max(top1[:, b, i], hb[2 + i][:, C:C + E]))
                after(n)
                nc.vector.tensor_tensor(dtop1[:, b], top1[:, b, :, 0], top1[:, b, :, 1], ALU.subtract).then_inc(dtop1_ready, 1)
                if b + 1 < B:
                    low_h1(b + 1)
                v.wait_ge(dth1_ready, b + 1)
                tick(nc.vector.tensor_scalar(rw[:, b, 0], dth1[:, b], 0.5, 0.5, ALU.mult, ALU.add))
                after(tick(nc.vector.tensor_scalar(rw[:, b, 1], dth1[:, b], -0.5, 0.5, ALU.mult, ALU.add)))
                nc.vector.tensor_tensor(rw[:, b, 2], rw[:, b, 0], rw[:, b, 1], ALU.add).then_inc(rw_ready, 1)
                if b == 0:
                    combine(b + 2)
                direct = b in (0, B - 1)
                if direct:
                    v.wait_ge(rw_ready, b + 1)
                    for i in range(TB):
                        n_ = b * TB + i
                        v.wait_ge(x1_ready, n_ + 1)
                        nc.vector.scalar_tensor_tensor(out=xt[:, n_], in0=hb[2 + i][:, 0:C], scalar=rw[:, b, 2, i:i + 1],
                                                       in1=xt[:, n_], op0=ALU.mult, op1=ALU.add).then_inc(ex_taken, 1)
                if 1 <= b < B - 2:
                    combine(b + 2)
                for i in range(TB):
                    n_ = b * TB + i
                    if direct:
                        v.wait_ge(ex_taken, n_ + 1)
                    else:
                        v.wait_ge(ex_added, n_ - TB + 1)
                    v.wait_ge(y_ready, n_ + 1)
                    nc.vector.tensor_tensor(xt[:, n_], dn[i][:, 0:C], xt[:, n_], ALU.add).then_inc(y_done, 1)

        @block.tensor
        def _(pe):
            def mm(dst, w, m, first, last):
                return nc.tensor.matmul(dst, w, m, start=first, stop=last)

            def split_mm(dst, w, m, first, last):
                mm(dst, w[0], m[0], first, False)
                mm(dst, w[0], m[1], False, False)
                return mm(dst, w[1], m[0], False, last)

            def turn_rows(b):
                pe.wait_ge(h0_ready, b + 1)
                if b >= 1:
                    pe.wait_ge(lg_ready, b * TB)
                for r in range(1, len(ROUNDS)):
                    if b == ROUNDS[r][0]:
                        pe.wait_ge(put_ready, r)
                for i in range(TB):
                    for c in range(CH):
                        at = c * P
                        last = nc.tensor.matmul(tp[i][:, at:at + P + E], xc[:, b, c, i * P:(i + 1) * P], turn[:, c],
                                                start=c == 0, stop=c == CH - 1, skip_group_check=True)
                last.then_inc(htp_ready, 1)

            def shared_up(u):
                _, b, j = chunks[u]
                if b == 0 and j % 2 == 0:
                    pe.wait_ge(ld_sup[j // 2], 16)
                if chunk_before(u):
                    pe.wait_ge(hid_ready, chunk_before(u))
                bank_ = hb[chunk_banks[u][0]]
                for half in range(2 if j < JC else 1):
                    for c in range(CH):
                        wcols = 2 * P if j < JC else 2 * JR
                        at = j * CH * 2 * P + c * wcols + half * P
                        last = mm(bank_[:, half * T:half * T + T], sup_s[:, at:at + P], xc[:, b, c], c == 0, c == CH - 1)
                last.then_inc(up_ready, 1)

            def shared_down(b, tiles=range(TB)):
                if b == 0:
                    pe.wait_ge(ld_sdn, 32)
                last_chunk = chunks.index(("shared", b, JC))
                pe.wait_ge(hid_ready, last_chunk)
                if b >= 2:
                    pe.wait_ge(sh_taken, b - 1)
                if b == B - 1:
                    pe.wait_ge(mo_taken, 2 * E)
                for i in tiles:
                    for j in range(NCHUNK):
                        rows = P if j < JC else JR
                        if j == JC and i == 0:
                            pe.wait_ge(hid_ready, last_chunk + 1)
                        last = mm(dn[b % 2][:, i * C:(i + 1) * C], hid[0:rows, b % 2, j, i * P:(i + 1) * P], sdn_s[0:rows, j],
                                  j == 0, j == NCHUNK - 1)
                if i == TB - 1:
                    last.then_inc(sh_ready, 1)

            def ranks(r):
                b0, b1 = ROUNDS[r]
                n0, n1 = b0 * TB, b1 * TB
                pe.wait_ge(hot_ready, r + 1)
                pe.wait_ge(lg_ready, b1 * TB)
                mm(tp[0][:, n0 * E:n1 * E], before[:], hot[:, n0:n1], True, n1 == 1)
                for n in range(n1 - 1):
                    lo = max(n + 1, n0)
                    last = mm(tp[0][:, lo * E:n1 * E], ones[:], hot[:, n:n + 1].to_broadcast([P, n1 - lo, E]), False, n == n1 - 2)
                last.then_inc(pos_ready, 1)

            pe.wait_ge(consts, 7 + E)
            pe.wait_ge(ld_router, 32)
            turn_rows(0)
            for u in range(nearly):
                for b, at in TURN_AT.items():
                    if u == at:
                        turn_rows(b)
                shared_up(u)
                for r in range(len(ROUNDS)):
                    if u == RANK_AT[r]:
                        ranks(r)
                if u in DOWN_BEHIND:
                    shared_down(DOWN_BEHIND.index(u))

            def slots_T(t):
                q, i = divmod(t, 3)
                if i < 2:
                    pe.wait_ge((ld_head, ld_buf)[i][q], 16)
                if t >= 2:
                    pe.wait_ge(bufT_ready, t - 1)
                else:
                    pe.wait_ge(put_ready, len(ROUNDS))
                n = min(2, 5 - 2 * i)
                for c in range(CH):
                    for k_ in range(n):
                        at = (c * n + k_) * P
                        last = nc.tensor.transpose(tp[t % 2][:, at:at + P], buf[:, q % 2, 2 * i + k_, c * P:(c + 1) * P], ident[:])
                last.then_inc(btp_ready, 1)

            def expert_up(e):
                pe.wait_ge(mup_ready, e + 1)
                pe.wait_ge(bufT_ready, 3 * (e // 2) + 2 + e % 2)
                for j in range(2):
                    u = nearly + 2 * e + j
                    pe.wait_ge(hid_ready, chunk_before(u))
                    for half in range(2 - j):
                        at, m = (half * IA, IA) if j == 0 else (2 * IA, 2 * IB)
                        for c in range(CH):
                            w = [mup_w[:, e % 2, part, c, at:at + m] for part in range(2)]
                            x_ = [bufT[:, (e // 2) % 2, part, c, (e % 2) * CAP:(e % 2 + 1) * CAP] for part in range(2)]
                            last = split_mm(hb[chunk_banks[u][half]][0:m, 0:CAP], w, x_, c == 0, c == CH - 1)
                    last.then_inc(up_ready, 1)

            def expert_down(e):
                if e == 0:
                    pe.wait_ge(sh_taken, B - 1)
                    pe.wait_ge(ld_mdn, 32)
                pe.wait_ge(hid_ready, nearly + 2 * e + 2)
                for r in range(3):
                    m = min(P, CAP - r * P)
                    if e >= 1 and r != 1:
                        pe.wait_ge(mo_taken, 2 * (e - 1) + (1 if r == 0 else 2))
                    for j, rows in enumerate((IA, IB)):
                        last = mm(dn[r // 2][0:m, (r % 2) * C:(r % 2 + 1) * C], hidm[0:rows, e % 2, j, r * P:r * P + m],
                                  mdn_s[0:rows, e, j], j == 0, j == 1)
                    if r >= 1:
                        last.then_inc(mo_ready, 1)

            for t in range(3):
                slots_T(t)
            for e in range(E + 1):
                turned_pair = e % 2 == 0 and e + 2 < E
                t = 3 * (e // 2 + 1)
                if e < E:
                    expert_up(e)
                if turned_pair:
                    slots_T(t)
                    slots_T(t + 1)
                if e % 2 == 1 and e + 1 < E:
                    slots_T(3 * (e + 1) // 2 + 2)
                if e >= 1:
                    expert_down(e - 1)

            for u in range(nlate, nchunks):
                shared_up(u)
            shared_down(B - 1, range(TB - 1))

            def turn_x1(b):
                if b >= 2:
                    pe.wait_ge(tanh1_done, b - 1)
                for i in range(TB):
                    pe.wait_ge(x1_ready, b * TB + i + 1)
                    for c in range(CH):
                        last = nc.tensor.transpose(tp[b % 2][:, c * T + i * P:c * T + (i + 1) * P], xt[:, b * TB + i, c * P:(c + 1) * P], ident[:])
                last.then_inc(x1T_ready, 1)

            pe.wait_ge(bufT_ready, 3 * (E // 2))
            turn_x1(0)
            shared_down(B - 1, range(TB - 1, TB))
            for b in range(B):
                pe.wait_ge(h1_ready, CH * (b + 1))
                if b == 0:
                    pe.wait_ge(l1_ready, 2)
                if b >= 2:
                    pe.wait_ge(hid1_ready, b - 1)
                for o in range(CH):
                    for c in range(CH):
                        at = c * C + o * P
                        last = split_mm(hb[b % 2][:, o * T:(o + 1) * T], [l1_w[:, part, at:at + P] for part in range(2)],
                                        [h1_w[:, b % 2, part, c] for part in range(2)], c == 0, c == CH - 1)
                last.then_inc(up1_ready, 1)
                if b + 1 < B:
                    turn_x1(b + 1)
                if b >= 1:
                    pe.wait_ge(ex_taken, b * TB)
                for i in range(TB):
                    for c in range(CH):
                        at = 2 * CH * C + c * (C + E)
                        last = split_mm(hb[2 + i][:, 0:C + E], [h1_w[:, b % 2, part, c, i * P:(i + 1) * P] for part in range(2)],
                                        [l1_w[:, part, at:at + C + E] for part in range(2)], c == 0, c == CH - 1)
                last.then_inc(ex_ready, 1)
                if b >= 1:
                    pe.wait_ge(y_done, b * TB)
                else:
                    pe.wait_ge(sh_taken, B)
                pe.wait_ge(hid1_ready, b + 1)
                for i in range(TB):
                    for c in range(CH):
                        at = CH * C + c * C
                        last = split_mm(dn[i][:, 0:C], [hid1_w[:, b % 2, part, c, i * P:(i + 1) * P] for part in range(2)],
                                        [l1_w[:, part, at:at + C] for part in range(2)], c == 0, c == CH - 1)
                    last.then_inc(y_ready, 1)


def rev(a):
    return a[:, ::-1]


def _lay_out(x, fside_BxSxS_0, cond_512, L0_cond_w, L0_cond_u, L0_ffn_router, L0_ffn_w_up_gate, L0_ffn_w_down,
             L0_ffn_shared_w_up_gate, L0_ffn_shared_w_down, L1_cond_w, L1_cond_u, L1_ffn_W_up, L1_ffn_W_down,
             L1_ffn_W_gate, L1_ffn_W_expert):
    import numpy as np

    def channels(a):
        return a.transpose(2, 0, 1).reshape(CH, P, B, T).transpose(1, 2, 0, 3)

    def rows(w):
        return w.reshape(CH, P, -1).transpose(1, 0, 2)

    g, u = L0_ffn_shared_w_up_gate[:, :J], L0_ffn_shared_w_up_gate[:, J:]
    sup = [rows(np.concatenate([g[:, j * P:(j + 1) * P], u[:, j * P:(j + 1) * P]], 1)).reshape(P, -1) for j in range(JC)]
    sup.append(rows(np.concatenate([u[:, JC * P:], g[:, JC * P:]], 1)).reshape(P, -1))
    m = L0_ffn_w_up_gate
    mg, mu = m[:, :, :I], m[:, :, I:]
    mup = np.concatenate([mg[..., :IA], mu[..., :IA], mu[..., IA:], mg[..., IA:]], 2)
    return {
        "x_cm": channels(x),
        "x_tm": x.reshape(NT, P, C).transpose(1, 0, 2),
        "k_cm": channels(fside_BxSxS_0),
        "cond": cond_512,
        "wu": np.stack([L0_cond_w, L1_cond_w, L0_cond_u, L1_cond_u]).reshape(4, CH, P).transpose(2, 0, 1),
        "router": rows(L0_ffn_router),
        "sup": np.concatenate(sup, 1),
        "sdn": L0_ffn_shared_w_down,
        "mup": mup.reshape(E, CH, P, 2 * I).transpose(2, 0, 1, 3),
        "mdn": L0_ffn_w_down,
        "l1w": np.concatenate([rows(w).reshape(P, -1) for w in (
            L1_ffn_W_up.T, L1_ffn_W_down.T, np.concatenate([L1_ffn_W_expert, L1_ffn_W_gate.T], 1))], 1),
    }


def kernel(**inputs):
    import numpy as np
    import concourse.bacc as bacc
    from concourse.bass_utils import run_bass_kernel_spmd

    arrays = {n: np.ascontiguousarray(a) for n, a in _lay_out(**{n: np.asarray(a) for n, a in inputs.items()}).items()}
    nc = bacc.Bacc("TRN2", target_bir_lowering=False, num_devices=1)
    args = {n: nc.dram_tensor(n, a.shape, F32, kind="ExternalInput").ap() for n, a in arrays.items()}
    out = nc.dram_tensor("out", (B * T, C), F32, kind="ExternalOutput").ap()
    adaln_ffn(nc, **args, out=out)
    r = run_bass_kernel_spmd(nc, [arrays], core_ids=[0])
    return r.results[0]["out"].reshape(B, T, C)
```
